# Optimizing a Trainium2 kernel written in Bass

```python
import numpy as np
import jax
import jax.numpy as jnp

def _softmax(x, axis=-1):
    return jax.nn.softmax(x, axis=axis)

def _gelu(x):
    return jax.nn.gelu(x, approximate=True)

def _silu(x):
    return jax.nn.silu(x)

def _sigmoid(x):
    return jax.nn.sigmoid(x)

def _layernorm(x, axis=-1, eps=1e-05):
    m = jnp.mean(x, axis=axis, keepdims=True)
    v = jnp.var(x, axis=axis, keepdims=True)
    return (x - m) / jnp.sqrt(v + eps)

def _scatter_add(tgt, idx, src, axis=0):
    return tgt.at[idx].add(src)

def _segment_sum(src, seg, n):
    return jax.ops.segment_sum(src, seg, n)
kernel_name = 'mk_xattn_seq_d1_seqx_r2_498fbf'

def setup_inputs(seed: int=0):
    np.random.seed(seed)
    _w = jnp.asarray

    def _rec_inputs():
        import jax
        import jax.numpy as jnp
        _rk = jax.random.key(seed)
        x = -0.0003929 + 0.9999 * jax.random.normal(jax.random.fold_in(_rk, 1), (64, 256, 512), jnp.float32)
        _lenS = 256 - jax.random.randint(jax.random.fold_in(_rk, 7), (64,), 0, max(1, 256 // 4) + 1, jnp.int32)
        _lenS2 = 256 - jax.random.randint(jax.random.fold_in(_rk, 8), (64,), 0, max(1, 256 // 4) + 1, jnp.int32)
        _ctx_768P = jax.random.normal(jax.random.fold_in(_rk, 11), (64, 16, 384), jnp.float32)
        _ctx_768c = jax.random.dirichlet(jax.random.fold_in(_rk, 511), 0.3 * jnp.ones((16,), jnp.float32), (64, 256))
        _ctx_768t = jnp.einsum('bsk,bkd->bsd', _ctx_768c, _ctx_768P)
        _ctx_768t = _ctx_768t * jax.lax.rsqrt(jnp.mean(jnp.square(_ctx_768t)) + 1e-12) * 0.953939
        ctx_768 = -5.15168e-05 + 0.999825 * (_ctx_768t + 0.3 * jax.random.normal(jax.random.fold_in(_rk, 611), (64, 256, 384), jnp.float32))
        return (x, ctx_768)
    x, ctx_768 = _rec_inputs()

    def _L0_xattn_setup():
        import jax, jax.numpy as jnp
        import numpy as np
        D_TEXT, D_AUDIO, D_HID = (512, 384, 512)
        EPS = 1e-05

        def layer_norm(x, gamma, beta):
            mu = jnp.mean(x, axis=-1, keepdims=True)
            var = jnp.mean(jnp.square(x - mu), axis=-1, keepdims=True)
            return (x - mu) * jax.lax.rsqrt(var + EPS) * gamma + beta
        key = jax.random.key(seed)
        ks = jax.random.split(key, 8)
        B, L, S = (16, 512, 1024)

        def xavier(k, shape):
            bound = np.sqrt(6.0 / (shape[0] + shape[1]))
            return jax.random.uniform(k, shape, jnp.float32, -bound, bound)
        return {'H_l': jax.random.normal(ks[0], (B, L, D_TEXT), jnp.float32), 'H_a': jax.random.normal(ks[1], (B, S, D_AUDIO), jnp.float32), 'W_text': xavier(ks[2], (D_TEXT, D_HID)), 'b_text': jnp.zeros((D_HID,), jnp.float32), 'W_audio': xavier(ks[3], (D_AUDIO, D_HID)), 'b_audio': jnp.zeros((D_HID,), jnp.float32), 'W_out': xavier(ks[4], (D_HID, D_HID)), 'b_out': jnp.zeros((D_HID,), jnp.float32), 'g1': jnp.ones((D_HID,), jnp.float32), 'beta1': jnp.zeros((D_HID,), jnp.float32), 'g2': jnp.ones((D_HID,), jnp.float32), 'beta2': jnp.zeros((D_HID,), jnp.float32), 'g_out': jnp.ones((D_HID,), jnp.float32), 'beta_out': jnp.zeros((D_HID,), jnp.float32)}
    _L0_xattn_all = _L0_xattn_setup()
    _L0_xattn_in = {k: v for k, v in _L0_xattn_all.items() if k in ('W_text', 'b_text', 'W_audio', 'b_audio', 'W_out', 'b_out', 'g1', 'beta1', 'g2', 'beta2', 'g_out', 'beta_out')}
    del _L0_xattn_all
    return {'x': x, 'ctx_768': ctx_768, 'L0_xattn_W_text': _L0_xattn_in['W_text'], 'L0_xattn_b_text': _L0_xattn_in['b_text'], 'L0_xattn_W_audio': _L0_xattn_in['W_audio'], 'L0_xattn_b_audio': _L0_xattn_in['b_audio'], 'L0_xattn_W_out': _L0_xattn_in['W_out'], 'L0_xattn_b_out': _L0_xattn_in['b_out'], 'L0_xattn_g1': _L0_xattn_in['g1'], 'L0_xattn_beta1': _L0_xattn_in['beta1'], 'L0_xattn_g2': _L0_xattn_in['g2'], 'L0_xattn_beta2': _L0_xattn_in['beta2'], 'L0_xattn_g_out': _L0_xattn_in['g_out'], 'L0_xattn_beta_out': _L0_xattn_in['beta_out']}

def reference(x, ctx_768, L0_xattn_W_text, L0_xattn_b_text, L0_xattn_W_audio, L0_xattn_b_audio, L0_xattn_W_out, L0_xattn_b_out, L0_xattn_g1, L0_xattn_beta1, L0_xattn_g2, L0_xattn_beta2, L0_xattn_g_out, L0_xattn_beta_out):
    import jax
    import jax.numpy as jnp

    def _L0_xattn_ref(H_l, H_a, W_text, b_text, W_audio, b_audio, W_out, b_out, g1, beta1, g2, beta2, g_out, beta_out):
        import jax, jax.numpy as jnp
        import numpy as np
        D_TEXT, D_AUDIO, D_HID = (512, 384, 512)
        EPS = 1e-05

        def layer_norm(x, gamma, beta):
            mu = jnp.mean(x, axis=-1, keepdims=True)
            var = jnp.mean(jnp.square(x - mu), axis=-1, keepdims=True)
            return (x - mu) * jax.lax.rsqrt(var + EPS) * gamma + beta
        text_p = jnp.einsum('bld,dh->blh', H_l, W_text) + b_text
        audio_p = jnp.einsum('bsd,dh->bsh', H_a, W_audio) + b_audio
        Q = layer_norm(text_p, g1, beta1)
        K = layer_norm(audio_p, g2, beta2)
        V = audio_p
        scale = 1.0 / np.sqrt(D_HID).astype(np.float32)
        scores = jnp.einsum('blh,bsh->bls', Q, K) * scale
        alpha = jax.nn.softmax(scores, axis=-1)
        H_hyper = jnp.einsum('bls,bsh->blh', alpha, V)
        H_hyper = jnp.einsum('blh,hk->blk', H_hyper, W_out) + b_out
        return layer_norm(H_hyper + H_l, g_out, beta_out)
    x = _L0_xattn_ref(x, ctx_768, L0_xattn_W_text, L0_xattn_b_text, L0_xattn_W_audio, L0_xattn_b_audio, L0_xattn_W_out, L0_xattn_b_out, L0_xattn_g1, L0_xattn_beta1, L0_xattn_g2, L0_xattn_beta2, L0_xattn_g_out, L0_xattn_beta_out)
    return x

_drawn_inputs = setup_inputs


def setup_inputs(seed=0):
    import zlib

    import numpy as np

    out = dict(_drawn_inputs(seed))
    spreads = {'L0_xattn_b_text': (0.0, 0.506),
     'L0_xattn_b_audio': (0.0, 0.1),
     'L0_xattn_b_out': (0.0, 0.1),
     'L0_xattn_g1': (1.0, 0.2),
     'L0_xattn_beta1': (0.0, 0.502),
     'L0_xattn_g2': (1.0, 0.2),
     'L0_xattn_beta2': (0.0, 0.8),
     'L0_xattn_g_out': (1.0, 0.2),
     'L0_xattn_beta_out': (0.0, 0.1)}
    factors = {}
    for name, (base, spread) in spreads.items():
        noise = np.random.default_rng([zlib.crc32(name.encode()), seed]).standard_normal(out[name].shape)
        drawn = base * np.exp(spread * noise) if base else spread * noise
        out[name] = jnp.asarray(drawn.astype(out[name].dtype))
    for name, factor in factors.items():
        out[name] = (out[name] * factor).astype(out[name].dtype)
    return out
```

```python
from contextlib import ExitStack

import numpy as np

import concourse.bass as bass
from concourse import mybir

F32 = mybir.dt.float32
F32R = mybir.dt.float32r
ALU = mybir.AluOpType
ACT = mybir.ActivationFunctionType
AX_X = mybir.AxisListType.X

P = 128
EPS = 1e-5


def cross_attention_kernel(nc, x, ctx, w_text, b_text, w_audio, b_audio, w_out, b_out,
                           g1, beta1, g2, beta2, g_out, beta_out, out):
    B, L, D = x.shape
    S, DC = ctx.shape[1], ctx.shape[2]
    H = w_text.shape[1]
    NB = 2
    N = B // NB
    DT, CT, HT = D // P, DC // P, H // P
    LT, ST = L // P, S // P
    T = NB * LT
    assert D == H == 4 * P and LT == ST == 2 and T == HT == DT and NB * L == 512 and N >= 4
    SCALE = float(1.0 / np.sqrt(np.float32(H)))

    x_v = x.rearrange("(i b) (t p) d -> i p (b t) d", b=NB, p=P)
    c_v = ctx.rearrange("(i b) (t p) d -> i p (b t) d", b=NB, p=P)
    out_v = out.rearrange("(i b) (t p) d -> i p (b t) d", b=NB, p=P)

    with ExitStack() as stack:
        def sb(name, shape, dt=F32):
            return stack.enter_context(nc.sbuf_tensor(name, shape, dt))

        def bank(name):
            return stack.enter_context(nc.psum_tensor(name, [P, 512], F32))

        def sem(name):
            return stack.enter_context(nc.semaphore(name))

        ident = sb("ident", [P, P])
        neg_half, neg_one = sb("neg_half", [P, 1]), sb("neg_one", [P, 1])
        wt_hi, wt_lo = sb("wt_hi", [P, DT, H], F32R), sb("wt_lo", [P, DT, H], F32R)
        wa_hi, wa_lo = sb("wa_hi", [P, CT, H], F32R), sb("wa_lo", [P, CT, H], F32R)
        wao_hi, wao_lo = sb("wao_hi", [P, CT, H], F32R), sb("wao_lo", [P, CT, H], F32R)
        bt_row, ba_row = sb("bt_row", [P, H]), sb("ba_row", [P, H])
        bao_row = sb("bao_row", [P, H])
        go_row, betao_row = sb("go_row", [P, H]), sb("betao_row", [P, H])
        ba_col = sb("ba_col", [P, HT])
        g1_col, beta1_col = sb("g1_col", [P, HT]), sb("beta1_col", [P, HT])
        g2_col, beta2_col = sb("g2_col", [P, HT]), sb("beta2_col", [P, HT])
        x_in, c_in = sb("x_in", [P, T, D]), sb("c_in", [P, T, DC])
        c_hi, c_lo = sb("c_hi", [P, T, DC], F32R), sb("c_lo", [P, T, DC], F32R)
        x_bias = sb("x_bias", [P, T, D])
        xT_hi, xT_lo = sb("xT_hi", [P, DT, T * P], F32R), sb("xT_lo", [P, DT, T * P], F32R)
        cT_hi, cT_lo = sb("cT_hi", [P, CT, T * P], F32R), sb("cT_lo", [P, CT, T * P], F32R)
        k_rows, q_rows = sb("k_rows", [P, T, H]), sb("q_rows", [P, T, H])
        full = sb("full", [P, HT, T * P])
        kT_hi, kT_lo = sb("kT_hi", [P, HT, T * P], F32R), sb("kT_lo", [P, HT, T * P], F32R)
        qT_hi, qT_lo = sb("qT_hi", [P, HT, T * P], F32R), sb("qT_lo", [P, HT, T * P], F32R)
        probs = sb("probs", [P, T, S])
        pT_hi, pT_lo = sb("pT_hi", [P, NB, ST * L], F32R), sb("pT_lo", [P, NB, ST * L], F32R)
        pcT_hi, pcT_lo = sb("pcT_hi", [P, CT, T * P], F32R), sb("pcT_lo", [P, CT, T * P], F32R)
        y_rows = sb("y_rows", [P, T, H])
        k_bn, q_bn, y_bn = (sb(f"{n}_bn", [P, T, 6]) for n in "kqy")
        k_mv, q_mv, y_mv = (sb(f"{n}_mv", [P, T, 2]) for n in "kqy")
        k_sc, q_sc, y_sc = (sb(f"{n}_sc", [P, T, 3]) for n in "kqy")
        row_max, neg_max = sb("row_max", [P, T]), sb("neg_max", [P, T])
        row_sum, row_inv = sb("row_sum", [P, T]), sb("row_inv", [P, T])

        wide = [bank(f"wide{t}") for t in range(T)]
        turn = [bank(f"turn{n}") for n in range(2)]
        score = [bank(f"score{b}") for b in range(NB)]

        wa_stage, wt_stage, wo_stage, waT_stage = k_rows, q_rows, y_rows, full

        wa_loaded, wo_loaded, wt_loaded = sem("wa_loaded"), sem("wo_loaded"), sem("wt_loaded")
        params_loaded = sem("params_loaded")
        x_loaded, c_loaded = sem("x_loaded"), sem("c_loaded")
        stored = [sem(f"stored{t}") for t in range(T)]
        passed = sem("passed")
        ident_zeroed, ident_made = sem("ident_zeroed"), sem("ident_made")
        wa_hi_made, wa_split = sem("wa_hi_made"), sem("wa_split")
        wt_hi_made, wt_split = sem("wt_hi_made"), sem("wt_split")
        waT_done, waT_copied = sem("waT_done"), sem("waT_copied")
        wao_done, wao_hi_made, wao_split = sem("wao_done"), sem("wao_hi_made"), sem("wao_split")
        bao_done, bao_made = sem("bao_done"), sem("bao_made")
        k_done, q_done, out_done = sem("k_done"), sem("q_done"), sem("out_done")
        xT_done, cT_done = sem("xT_done"), sem("cT_done")
        kT_done, qT_done, pT_done = sem("kT_done"), sem("qT_done"), sem("pT_done")
        score_done, pc_done = sem("score_done"), sem("pc_done")
        xT_hi_made, cT_hi_made = sem("xT_hi_made"), sem("cT_hi_made")
        k_normed, q_normed, y_normed = sem("k_normed"), sem("q_normed"), sem("y_normed")
        k_full, q_full = sem("k_full"), sem("q_full")
        probs_made, pT_hi_made, pc_hi_made = sem("probs_made"), sem("pT_hi_made"), sem("pc_hi_made")
        xT_split, cT_split, pT_split, pc_split = sem("xT_split"), sem("cT_split"), sem("pT_split"), sem("pc_split")
        k_biased, q_biased, y_summed = sem("k_biased"), sem("q_biased"), sem("y_summed")
        k_stats, q_stats, y_stats = sem("k_stats"), sem("q_stats"), sem("y_stats")
        k_moments, q_moments, y_moments = sem("k_moments"), sem("q_moments"), sem("y_moments")
        kT_hi_made, kT_split = sem("kT_hi_made"), sem("kT_split")
        qT_hi_made, qT_split = sem("qT_hi_made"), sem("qT_split")
        max_made, neg_max_made, sums_inverted = sem("max_made"), sem("neg_max_made"), sem("sums_inverted")
        k_var, q_var, y_var = sem("k_var"), sem("q_var"), sem("y_var")
        k_rstd, q_rstd, y_rstd = sem("k_rstd"), sem("q_rstd"), sem("y_rstd")
        k_scales, q_scales, y_scales = sem("k_scales"), sem("q_scales"), sem("y_scales")
        c_hi_made, c_split, x_biased = sem("c_hi_made"), sem("c_split"), sem("x_biased")
        y_scaled, y_ready = sem("y_scaled"), sem("y_ready")

        def wait(eng, semaphore, value):
            if not isinstance(value, int) or value > 0:
                eng.wait_ge(semaphore, value)

        def wait_apart(eng, semaphore, value):
            if not isinstance(value, int) or value > 0:
                eng.wait_ge(semaphore, value)
                eng.sem_inc(passed, 1)

        def run_steps(eng, step):
            step(0, first=True)
            step(1)
            with eng.Fori(2, N - 1) as i:
                step(i)
            step(N - 1, last=True)

        block = stack.enter_context(nc.Block())

        @block.sync
        def _(sp):
            def load_c(i):
                sp.dma_start(c_in[:], c_v[i]).then_inc(c_loaded, 16)

            def load_x(i, t):
                sp.dma_start(x_in[:, t, :], x_v[i, :, t, :]).then_inc(x_loaded, 16)

            sp.dma_start(wa_stage[:, 0:CT, :], w_audio.rearrange("(t p) h -> p t h", p=P)).then_inc(wa_loaded, 16)
            load_c(0)
            sp.dma_start(wo_stage[:], w_out.rearrange("(t p) h -> p t h", p=P)).then_inc(wo_loaded, 16)
            columns = [(ba_col, b_audio), (g1_col, g1), (beta1_col, beta1), (g2_col, g2), (beta2_col, beta2)]
            rows = [(ba_row, b_audio), (bt_row, b_text), (bao_row, b_out), (go_row, g_out), (betao_row, beta_out)]
            for to, of in columns:
                sp.dma_start(to[:], of.rearrange("(t p) -> p t", p=P), allow_slow_non_contiguous=True).then_inc(params_loaded, 16)
            for to, of in rows:
                sp.dma_start(to[:], of.partition_broadcast(P)).then_inc(params_loaded, 16)
            sp.dma_start(wt_stage[:], w_text.rearrange("(t p) h -> p t h", p=P)).then_inc(wt_loaded, 16)
            for t in range(T):
                load_x(0, t)

            def store_y(j, t):
                wait_apart(sp, y_ready, T * j + t + 1)
                sp.dma_start(out_v[j, :, t, :], y_rows[:, t, :]).then_inc(stored[t], 16)

            def step(i, first=False, last=False):
                if not isinstance(i, int) or i >= 2:
                    store_y(i - 2, 2)
                    store_y(i - 2, 3)
                if not last:
                    wait_apart(sp, cT_done, CT * (i + 1))
                    wait_apart(sp, c_split, T * (i + 1))
                    load_c(i + 1)
                    wait_apart(sp, xT_done, DT * (i + 1))
                for t in range(T):
                    if not last:
                        wait_apart(sp, x_biased, T * i + t + 1)
                        load_x(i + 1, t)
                    if not first and t in (1, 2):
                        store_y(i - 1, t - 1)

            run_steps(sp, step)
            store_y(N - 2, 2)
            store_y(N - 2, 3)
            for t in range(T):
                store_y(N - 1, t)
            for t in range(T):
                sp.wait_ge(stored[t], 16 * N)

        @block.tensor
        def _(pe):
            def product(to, terms):
                n = len(terms)
                for m, (a_hi, a_lo, b_hi, b_lo) in enumerate(terms):
                    nc.tensor.matmul(to, a_hi, b_hi, start=(m == 0), stop=False)
                    nc.tensor.matmul(to, a_hi, b_lo, start=False, stop=False)
                    done = nc.tensor.matmul(to, a_lo, b_hi, start=False, stop=(m == n - 1))
                return done

            def transposes(to, blocks):
                for m, b in enumerate(blocks):
                    done = nc.tensor.transpose(to[:, m * P:(m + 1) * P], b, ident[:])
                return done

            def project_k(i, t):
                if t == 0:
                    pe.wait_ge(cT_split, CT * (i + 1))
                wait(pe, y_summed, T * (i - 2) + t + 1)
                rows = slice(t * P, (t + 1) * P)
                product(wide[t][:], [(cT_hi[:, d, rows], cT_lo[:, d, rows], wa_hi[:, d, :], wa_lo[:, d, :])
                                     for d in range(CT)]).then_inc(k_done, 1)

            def project_q(i, t):
                if t == 0:
                    pe.wait_ge(xT_split, DT * (i + 1))
                pe.wait_ge(k_biased, T * i + t + 1)
                rows = slice(t * P, (t + 1) * P)
                product(wide[t][:], [(xT_hi[:, d, rows], xT_lo[:, d, rows], wt_hi[:, d, :], wt_lo[:, d, :])
                                     for d in range(DT)]).then_inc(q_done, 1)

            def turn_x(i, d):
                if d == 0:
                    pe.wait_ge(x_loaded, 16 * T * (i + 1))
                transposes(turn[d % 2], [x_in[:, t, d * P:(d + 1) * P] for t in range(T)]).then_inc(xT_done, 1)

            def turn_c(i, d):
                if d == 0:
                    pe.wait_ge(c_loaded, 16 * (i + 1))
                transposes(turn[(d + 1) % 2], [c_in[:, t, d * P:(d + 1) * P] for t in range(T)]).then_inc(cT_done, 1)

            def turn_k(i, h):
                if h == 0:
                    pe.wait_ge(k_normed, T * (i + 1))
                transposes(turn[(h + 1) % 2], [k_rows[:, t, h * P:(h + 1) * P] for t in range(T)]).then_inc(kT_done, 1)

            def turn_q(i, h):
                if h == 0:
                    pe.wait_ge(q_normed, T * (i + 1))
                transposes(turn[(h + 1) % 2], [q_rows[:, t, h * P:(h + 1) * P] for t in range(T)]).then_inc(qT_done, 1)

            def turn_p(j, b):
                pe.wait_ge(probs_made, T * j + LT * (b + 1))
                transposes(turn[b], [probs[:, LT * b + l, s * P:(s + 1) * P] for s in range(ST) for l in range(LT)]
                           ).then_inc(pT_done, 1)

            def scores(i, b, l):
                at = LT * b + l
                rows, keys = slice(at * P, (at + 1) * P), slice(b * S, (b + 1) * S)
                done = product(score[b][:, l * S:(l + 1) * S],
                               [(qT_hi[:, h, rows], qT_lo[:, h, rows], kT_hi[:, h, keys], kT_lo[:, h, keys])
                                for h in range(HT)])
                if l == LT - 1:
                    done.then_inc(score_done, 1)

            def probs_context(j, d):
                if d == 0:
                    pe.wait_ge(c_split, T * (j + 1))
                    pe.wait_ge(pT_split, NB * (j + 1))
                to = (score[0], score[1], turn[0])[d]
                cols = slice(d * P, (d + 1) * P)
                for b in range(NB):
                    done = product(to[:, b * L:(b + 1) * L],
                                   [(c_hi[:, ST * b + s, cols], c_lo[:, ST * b + s, cols],
                                     pT_hi[:, b, s * L:(s + 1) * L], pT_lo[:, b, s * L:(s + 1) * L])
                                    for s in range(ST)])
                done.then_inc(pc_done, 1)

            def output(j, t):
                if t == 0:
                    pe.wait_ge(pc_split, CT * (j + 1))
                rows = slice(t * P, (t + 1) * P)
                product(wide[t][:], [(pcT_hi[:, d, rows], pcT_lo[:, d, rows], wao_hi[:, d, :], wao_lo[:, d, :])
                                     for d in range(CT)]).then_inc(out_done, 1)

            pe.wait_ge(ident_made, 1)
            pe.wait_ge(wa_loaded, 16)
            for h in range(HT):
                transposes(wide[h], [wa_stage[:, d, h * P:(h + 1) * P] for d in range(CT)]).then_inc(waT_done, 1)
            turn_c(0, 0)
            turn_c(0, 1)
            pe.wait_ge(cT_split, 1)
            turn_c(0, 2)
            pe.wait_ge(waT_copied, HT)
            pe.wait_ge(wo_loaded, 16)
            for d in range(CT):
                for h in range(HT):
                    done = nc.tensor.matmul(wide[d][:], waT_stage[:, h, d * P:(d + 1) * P], wo_stage[:, h, :],
                                            start=(h == 0), stop=(h == HT - 1))
                done.then_inc(wao_done, 1)
            pe.wait_ge(params_loaded, 16 * 10)
            for h in range(HT):
                done = nc.tensor.matmul(wide[CT][:], ba_col[:, h:h + 1].broadcast_to([P, P]), wo_stage[:, h, :],
                                        start=(h == 0), stop=(h == HT - 1))
            done.then_inc(bao_done, 1)
            pe.wait_ge(wa_split, CT)
            pe.wait_ge(wao_split, CT)
            pe.wait_ge(bao_made, 1)

            def step(i, first=False, last=False):
                j = i - 1
                project_k(i, 0)
                if not first:
                    turn_p(j, 0)
                project_k(i, 1)
                if not first:
                    turn_p(j, 1)
                    pe.wait_ge(pT_split, NB * j + 1)
                turn_x(i, 0)
                project_k(i, 2)
                if not first:
                    pe.wait_ge(pT_split, NB * j + 2)
                turn_x(i, 1)
                project_k(i, 3)
                pe.wait_ge(xT_split, DT * i + 1)
                turn_x(i, 2)
                if not first:
                    probs_context(j, 0)
                pe.wait_ge(xT_split, DT * i + 2)
                turn_x(i, 3)
                if not first:
                    probs_context(j, 1)
                pe.wait_ge(xT_split, DT * i + 3)
                if not first:
                    probs_context(j, 2)
                if first:
                    pe.wait_ge(wt_split, DT)
                project_q(i, 0)
                turn_k(i, 0)
                project_q(i, 1)
                if not first:
                    pe.wait_ge(pc_split, CT * (j + 1))
                turn_k(i, 1)
                project_q(i, 2)
                pe.wait_ge(k_full, HT * i + 1)
                turn_k(i, 2)
                project_q(i, 3)
                pe.wait_ge(k_full, HT * i + 2)
                turn_k(i, 3)
                if not first:
                    pe.wait_ge(q_biased, T * i + 1)
                    output(j, 0)
                    pe.wait_ge(q_biased, T * i + 2)
                    output(j, 1)
                pe.wait_ge(k_full, HT * i + 3)
                turn_q(i, 0)
                pe.wait_ge(k_full, HT * i + 4)
                turn_q(i, 1)
                if not first:
                    pe.wait_ge(q_biased, T * i + 3)
                    output(j, 2)
                pe.wait_ge(q_full, HT * i + 1)
                turn_q(i, 2)
                pe.wait_ge(q_full, HT * i + 2)
                turn_q(i, 3)
                if not first:
                    pe.wait_ge(q_biased, T * i + 4)
                    output(j, 3)
                if not last:
                    pe.wait_ge(q_full, HT * i + 3)
                    turn_c(i + 1, 0)
                pe.wait_ge(kT_split, HT * (i + 1))
                pe.wait_ge(qT_split, HT * (i + 1))
                scores(i, 0, 0)
                if not last:
                    pe.wait_ge(q_full, HT * i + 4)
                    turn_c(i + 1, 1)
                scores(i, 0, 1)
                if not last:
                    pe.wait_ge(cT_split, CT * (i + 1) + 1)
                    turn_c(i + 1, 2)
                scores(i, 1, 0)
                scores(i, 1, 1)

            run_steps(pe, step)
            turn_p(N - 1, 0)
            turn_p(N - 1, 1)
            for d in range(CT):
                probs_context(N - 1, d)
            for t in range(T):
                output(N - 1, t)

        @block.scalar
        def _(act):
            def xT_high(i, d):
                act.wait_ge(xT_done, DT * i + d + 1)
                wait(act, q_done, T * i)
                nc.scalar.copy(xT_hi[:, d, :], turn[d % 2][:]).then_inc(xT_hi_made, 1)

            def cT_high(i, d):
                act.wait_ge(cT_done, CT * i + d + 1)
                wait(act, k_done, T * i)
                nc.scalar.copy(cT_hi[:, d, :], turn[(d + 1) % 2][:]).then_inc(cT_hi_made, 1)

            def pT_high(j, b):
                act.wait_ge(pT_done, NB * j + b + 1)
                wait(act, pc_done, CT * j)
                nc.scalar.copy(pT_hi[:, b, :], turn[b][:]).then_inc(pT_hi_made, 1)

            def pc_high(j, d):
                act.wait_ge(pc_done, CT * j + d + 1)
                wait(act, out_done, T * j)
                of = (score[0], score[1], turn[0])[d]
                nc.scalar.copy(pcT_hi[:, d, :], of[:]).then_inc(pc_hi_made, 1)

            def k_norm(i, t):
                act.wait_ge(k_scales, T * i + t + 1)
                nc.scalar.activation(k_rows[:, t, :], k_rows[:, t, :], ACT.Identity,
                                     scale=k_sc[:, t, 0:1], bias=k_sc[:, t, 1:2]).then_inc(k_normed, 1)

            def q_norm(i, t):
                act.wait_ge(q_scales, T * i + t + 1)
                nc.scalar.activation(q_rows[:, t, :], q_rows[:, t, :], ACT.Identity,
                                     scale=q_sc[:, t, 0:1], bias=q_sc[:, t, 1:2]).then_inc(q_normed, 1)

            def y_norm(j, t):
                act.wait_ge(y_scales, T * j + t + 1)
                nc.scalar.activation(y_rows[:, t, :], y_rows[:, t, :], ACT.Identity,
                                     scale=y_sc[:, t, 0:1], bias=y_sc[:, t, 1:2]).then_inc(y_normed, 1)

            def k_affine(i, h):
                act.wait_ge(kT_done, HT * i + h + 1)
                wait(act, qT_split, HT * (i - 1) + h + 1)
                nc.scalar.activation(full[:, h, :], turn[(h + 1) % 2][:], ACT.Identity,
                                     scale=g2_col[:, h:h + 1], bias=beta2_col[:, h:h + 1]).then_inc(k_full, 1)

            def q_affine(i, h):
                act.wait_ge(qT_done, HT * i + h + 1)
                act.wait_ge(kT_split, HT * i + h + 1)
                nc.scalar.activation(full[:, h, :], turn[(h + 1) % 2][:], ACT.Identity,
                                     scale=g1_col[:, h:h + 1], bias=beta1_col[:, h:h + 1]).then_inc(q_full, 1)

            def exponentials(i, b):
                act.wait_ge(neg_max_made, NB * i + b + 1)
                wait(act, pT_done, NB * (i - 1) + b + 1)
                wait(act, sums_inverted, i)
                for l in range(LT):
                    at = LT * b + l
                    nc.scalar.activation(probs[:, at, :], score[b][:, l * S:(l + 1) * S], ACT.Exp,
                                         scale=SCALE, bias=neg_max[:, at:at + 1],
                                         accum_out=row_sum[:, at:at + 1]).then_inc(probs_made, 1)

            for h in range(HT):
                act.wait_ge(waT_done, h + 1)
                nc.scalar.copy(waT_stage[:, h, 0:DC], wide[h][:, 0:DC]).then_inc(waT_copied, 1)
            for d in range(CT):
                cT_high(0, d)
            for d in range(CT):
                act.wait_ge(wao_done, d + 1)
                nc.scalar.copy(wao_hi[:, d, :], wide[d][:]).then_inc(wao_hi_made, 1)
            act.wait_ge(params_loaded, 16 * 10)

            def step(i, first=False, last=False):
                j = i - 1
                if not first:
                    pT_high(j, 0)
                    pT_high(j, 1)
                xT_high(i, 0)
                k_norm(i, 0)
                xT_high(i, 1)
                k_norm(i, 1)
                xT_high(i, 2)
                k_norm(i, 2)
                if not first:
                    pc_high(j, 0)
                xT_high(i, 3)
                k_norm(i, 3)
                if not first:
                    pc_high(j, 1)
                    pc_high(j, 2)
                k_affine(i, 0)
                q_norm(i, 0)
                k_affine(i, 1)
                q_norm(i, 1)
                k_affine(i, 2)
                q_norm(i, 2)
                k_affine(i, 3)
                q_norm(i, 3)
                q_affine(i, 0)
                q_affine(i, 1)
                if not first:
                    y_norm(j, 0)
                    y_norm(j, 1)
                q_affine(i, 2)
                q_affine(i, 3)
                if not last:
                    cT_high(i + 1, 0)
                if not first:
                    y_norm(j, 2)
                if not last:
                    cT_high(i + 1, 1)
                if not first:
                    y_norm(j, 3)
                if not last:
                    cT_high(i + 1, 2)
                exponentials(i, 0)
                exponentials(i, 1)

            run_steps(act, step)
            for b in range(NB):
                pT_high(N - 1, b)
            for d in range(CT):
                pc_high(N - 1, d)
            for t in range(T):
                y_norm(N - 1, t)

        @block.vector
        def _(dve):
            def low(to, whole, hi):
                return nc.vector.tensor_tensor(to, whole, hi.bitcast(F32), ALU.subtract)

            def xT_low(i, d):
                dve.wait_ge(xT_hi_made, DT * i + d + 1)
                low(xT_lo[:, d, :], turn[d % 2][:], xT_hi[:, d, :]).then_inc(xT_split, 1)

            def cT_low(i, d):
                dve.wait_ge(cT_hi_made, CT * i + d + 1)
                low(cT_lo[:, d, :], turn[(d + 1) % 2][:], cT_hi[:, d, :]).then_inc(cT_split, 1)

            def pT_low(j, b):
                dve.wait_ge(pT_hi_made, NB * j + b + 1)
                low(pT_lo[:, b, :], turn[b][:], pT_hi[:, b, :]).then_inc(pT_split, 1)

            def pc_low(j, d):
                dve.wait_ge(pc_hi_made, CT * j + d + 1)
                of = (score[0], score[1], turn[0])[d]
                low(pcT_lo[:, d, :], of[:], pcT_hi[:, d, :]).then_inc(pc_split, 1)

            def k_bias(i, t):
                dve.wait_ge(k_done, T * i + t + 1)
                if t == 0:
                    wait(dve, kT_done, HT * i)
                nc.vector.tensor_tensor(k_rows[:, t, :], wide[t][:], ba_row[:], ALU.add).then_inc(k_biased, 1)
                dve.wait_ge(k_biased, T * i + t + 1)
                nc.vector.bn_stats(k_bn[:, t, :], k_rows[:, t, :]).then_inc(k_stats, 1)
                wait_apart(dve, k_stats, T * i + t + 1)
                nc.vector.bn_aggr(k_mv[:, t, :], k_bn[:, t, :]).then_inc(k_moments, 1)

            def q_bias(i, t):
                dve.wait_ge(q_done, T * i + t + 1)
                if t == 0:
                    wait(dve, qT_done, HT * i)
                nc.vector.tensor_tensor(q_rows[:, t, :], wide[t][:], bt_row[:], ALU.add).then_inc(q_biased, 1)
                dve.wait_ge(q_biased, T * i + t + 1)
                nc.vector.bn_stats(q_bn[:, t, :], q_rows[:, t, :]).then_inc(q_stats, 1)
                wait_apart(dve, q_stats, T * i + t + 1)
                nc.vector.bn_aggr(q_mv[:, t, :], q_bn[:, t, :]).then_inc(q_moments, 1)

            def y_sum(j, t):
                dve.wait_ge(out_done, T * j + t + 1)
                dve.wait_ge(x_biased, T * j + t + 1)
                dve.wait_ge(sums_inverted, j + 1)
                wait(dve, stored[t], 16 * j)
                nc.vector.scalar_tensor_tensor(out=y_rows[:, t, :], in0=wide[t][:], scalar=row_inv[:, t:t + 1],
                                               in1=x_bias[:, t, :], op0=ALU.mult, op1=ALU.add).then_inc(y_summed, 1)
                dve.wait_ge(y_summed, T * j + t + 1)
                nc.vector.bn_stats(y_bn[:, t, :], y_rows[:, t, :]).then_inc(y_stats, 1)
                wait_apart(dve, y_stats, T * j + t + 1)
                nc.vector.bn_aggr(y_mv[:, t, :], y_bn[:, t, :]).then_inc(y_moments, 1)

            def k_halves(i, h):
                dve.wait_ge(k_full, HT * i + h + 1)
                if h == 0:
                    wait(dve, score_done, NB * i)
                nc.vector.tensor_copy(kT_hi[:, h, :], full[:, h, :]).then_inc(kT_hi_made, 1)
                dve.wait_ge(kT_hi_made, HT * i + h + 1)
                low(kT_lo[:, h, :], full[:, h, :], kT_hi[:, h, :]).then_inc(kT_split, 1)

            def q_halves(i, h):
                dve.wait_ge(q_full, HT * i + h + 1)
                nc.vector.tensor_copy(qT_hi[:, h, :], full[:, h, :]).then_inc(qT_hi_made, 1)
                dve.wait_ge(qT_hi_made, HT * i + h + 1)
                low(qT_lo[:, h, :], full[:, h, :], qT_hi[:, h, :]).then_inc(qT_split, 1)

            def maxima(i, b):
                tiles = slice(LT * b, LT * (b + 1))
                dve.wait_ge(score_done, NB * i + b + 1)
                nc.vector.reduce_max(row_max[:, tiles], score[b][:].rearrange("p (l s) -> p l s", l=LT),
                                     AX_X).then_inc(max_made, 1)
                dve.wait_ge(max_made, NB * i + b + 1)
                nc.vector.tensor_scalar(neg_max[:, tiles], row_max[:, tiles], -SCALE, None,
                                        ALU.mult).then_inc(neg_max_made, 1)

            def invert_sums(j):
                dve.wait_ge(probs_made, T * (j + 1))
                nc.vector.reciprocal(row_inv[:], row_sum[:]).then_inc(sums_inverted, 1)

            def split_weights(to_hi, to_lo, of, n, hi_made, split):
                for d in range(n):
                    nc.vector.tensor_copy(to_hi[:, d, :], of[:, d, :]).then_inc(hi_made, 1)
                for d in range(n):
                    dve.wait_ge(hi_made, d + 1)
                    low(to_lo[:, d, :], of[:, d, :], to_hi[:, d, :]).then_inc(split, 1)

            dve.wait_ge(wa_loaded, 16)
            split_weights(wa_hi, wa_lo, wa_stage, CT, wa_hi_made, wa_split)
            for d in range(CT):
                cT_low(0, d)
            dve.wait_ge(wt_loaded, 16)
            split_weights(wt_hi, wt_lo, wt_stage, DT, wt_hi_made, wt_split)
            for d in range(CT):
                dve.wait_ge(wao_hi_made, d + 1)
                low(wao_lo[:, d, :], wide[d][:], wao_hi[:, d, :]).then_inc(wao_split, 1)
            dve.wait_ge(bao_done, 1)
            dve.wait_ge(params_loaded, 16 * 10)
            nc.vector.tensor_tensor(bao_row[:], wide[CT][:], bao_row[:], ALU.add).then_inc(bao_made, 1)

            def step(i, first=False, last=False):
                j = i - 1
                if not first:
                    invert_sums(j)
                k_bias(i, 0)
                if not first:
                    pT_low(j, 0)
                k_bias(i, 1)
                if not first:
                    pT_low(j, 1)
                xT_low(i, 0)
                k_bias(i, 2)
                xT_low(i, 1)
                k_bias(i, 3)
                xT_low(i, 2)
                if not first:
                    pc_low(j, 0)
                xT_low(i, 3)
                if not first:
                    pc_low(j, 1)
                    pc_low(j, 2)
                for t in range(T):
                    q_bias(i, t)
                    k_halves(i, t)
                if not first:
                    y_sum(j, 0)
                    y_sum(j, 1)
                q_halves(i, 0)
                q_halves(i, 1)
                if not first:
                    y_sum(j, 2)
                q_halves(i, 2)
                q_halves(i, 3)
                if not first:
                    y_sum(j, 3)
                if not last:
                    cT_low(i + 1, 0)
                    cT_low(i + 1, 1)
                    maxima(i, 0)
                    cT_low(i + 1, 2)
                else:
                    maxima(i, 0)
                maxima(i, 1)

            run_steps(dve, step)
            invert_sums(N - 1)
            for b in range(NB):
                pT_low(N - 1, b)
            for d in range(CT):
                pc_low(N - 1, d)
            for t in range(T):
                y_sum(N - 1, t)

        @block.gpsimd
        def _(pool):
            def scales(i, t, moments, mv, sc, var, rstd, made):
                at = T * i + t + 1
                wait_apart(pool, moments, at)
                nc.gpsimd.tensor_scalar(sc[:, t, 2:3], mv[:, t, 1:2], EPS, 1.0, ALU.add, ALU.mult).then_inc(var, 1)
                pool.wait_ge(var, at)
                nc.gpsimd.tensor_tensor(sc[:, t, 0:1], sc[:, t, 2:3], neg_half[:], ALU.pow).then_inc(rstd, 1)
                wait_apart(pool, rstd, at)
                nc.gpsimd.tensor_scalar(sc[:, t, 1:2], mv[:, t, 0:1], sc[:, t, 0:1], neg_one[:, 0:1],
                                        ALU.mult, ALU.mult).then_inc(made, 1)

            def k_scale(i, t):
                scales(i, t, k_moments, k_mv, k_sc, k_var, k_rstd, k_scales)

            def q_scale(i, t):
                scales(i, t, q_moments, q_mv, q_sc, q_var, q_rstd, q_scales)

            def y_scale(j, t):
                scales(j, t, y_moments, y_mv, y_sc, y_var, y_rstd, y_scales)

            def split_c(i, t):
                if t == 0:
                    wait_apart(pool, c_loaded, 16 * (i + 1))
                    wait_apart(pool, pc_done, CT * i)
                nc.gpsimd.tensor_scalar(c_hi[:, t, :], c_in[:, t, :], 1.0, 1.0, ALU.mult,
                                        ALU.mult).then_inc(c_hi_made, 1)
                pool.wait_ge(c_hi_made, T * i + t + 1)
                nc.gpsimd.tensor_tensor(c_lo[:, t, :], c_in[:, t, :], c_hi[:, t, :].bitcast(F32),
                                        ALU.subtract).then_inc(c_split, 1)

            def bias_x(i, t):
                if t == 0:
                    pool.wait_ge(x_loaded, 16 * T * (i + 1))
                wait(pool, y_summed, T * (i - 1) + t + 1)
                nc.gpsimd.tensor_tensor(x_bias[:, t, :], x_in[:, t, :], bao_row[:], ALU.add).then_inc(x_biased, 1)

            def finish_y(j, t):
                pool.wait_ge(y_normed, T * j + t + 1)
                nc.gpsimd.tensor_tensor(y_rows[:, t, :], y_rows[:, t, :], go_row[:], ALU.mult).then_inc(y_scaled, 1)
                pool.wait_ge(y_scaled, T * j + t + 1)
                nc.gpsimd.tensor_tensor(y_rows[:, t, :], y_rows[:, t, :], betao_row[:], ALU.add).then_inc(y_ready, 1)

            nc.gpsimd.memset(ident[:], 0.0).then_inc(ident_zeroed, 1)
            nc.gpsimd.memset(neg_half[:], -0.5).then_inc(ident_zeroed, 1)
            nc.gpsimd.memset(neg_one[:], -1.0).then_inc(ident_zeroed, 1)
            pool.wait_ge(ident_zeroed, 3)
            nc.gpsimd.affine_select(out=ident[:], in_=ident[:], compare_op=ALU.not_equal, fill=1.0, base=0,
                                    pattern=[[-1, P]], channel_multiplier=1).then_inc(ident_made, 1)

            def step(i, first=False, last=False):
                j = i - 1
                finish_late = not isinstance(i, int) or i >= 2
                k_scale(i, 0)
                if finish_late:
                    finish_y(i - 2, 2)
                k_scale(i, 1)
                if finish_late:
                    finish_y(i - 2, 3)
                k_scale(i, 2)
                k_scale(i, 3)
                split_c(i, 0)
                split_c(i, 1)
                q_scale(i, 0)
                split_c(i, 2)
                q_scale(i, 1)
                split_c(i, 3)
                q_scale(i, 2)
                q_scale(i, 3)
                if first:
                    pool.wait_ge(bao_made, 1)
                for t in range(T):
                    if not first:
                        y_scale(j, t)
                    bias_x(i, t)
                    if not first and t in (1, 2):
                        finish_y(j, t - 1)

            run_steps(pool, step)
            for t in (2, 3):
                finish_y(N - 2, t)
            for t in range(T):
                y_scale(N - 1, t)
                finish_y(N - 1, t)


_INS = ["x", "ctx_768", "L0_xattn_W_text", "L0_xattn_b_text", "L0_xattn_W_audio", "L0_xattn_b_audio",
        "L0_xattn_W_out", "L0_xattn_b_out", "L0_xattn_g1", "L0_xattn_beta1", "L0_xattn_g2", "L0_xattn_beta2",
        "L0_xattn_g_out", "L0_xattn_beta_out"]


def kernel(**inputs):
    import numpy as _np
    import concourse.bacc as _bacc
    from concourse import mybir as _mybir
    from concourse.bass_utils import run_bass_kernel_spmd as _run

    nc = _bacc.Bacc("TRN2", target_bir_lowering=False, num_devices=1)
    arrays, args = {}, []
    for name in _INS:
        a = _np.ascontiguousarray(inputs[name])
        arrays[f"in_{name}"] = a
        args.append(nc.dram_tensor(f"in_{name}", a.shape, _mybir.dt.from_np(a.dtype), kind="ExternalInput").ap())
    out = nc.dram_tensor("out", arrays["in_x"].shape, _mybir.dt.float32, kind="ExternalOutput").ap()
    cross_attention_kernel(nc, *args, out)
    r = _run(nc, [arrays], core_ids=[0])
    return r.results[0]["out"]
```

```python
from contextlib import ExitStack

import numpy as np

import concourse.bass as bass
from concourse import mybir

F32 = mybir.dt.float32
F32R = mybir.dt.float32r
ALU = mybir.AluOpType
ACT = mybir.ActivationFunctionType
AX_X = mybir.AxisListType.X

P = 128
EPS = 1e-5


def cross_attention_kernel(nc, x, ctx, w_text, b_text, w_audio, b_audio, w_out, b_out,
                           g1, beta1, g2, beta2, g_out, beta_out, out):
    B, L, D = x.shape
    S, DC = ctx.shape[1], ctx.shape[2]
    H = w_text.shape[1]
    NB = 2
    N = B // NB
    DT, CT, HT = D // P, DC // P, H // P
    LT, ST = L // P, S // P
    T = NB * LT
    assert D == H == 4 * P and LT == ST == 2 and T == HT == DT and NB * L == 512 and N >= 6 and N % 2 == 0
    SCALE = float(1.0 / np.sqrt(np.float32(H)))

    x_v = x.rearrange("(i b) (t p) d -> i p (b t) d", b=NB, p=P)
    c_v = ctx.rearrange("(i b) (t p) d -> i p (b t) d", b=NB, p=P)
    out_v = out.rearrange("(i b) (t p) d -> i p (b t) d", b=NB, p=P)

    with ExitStack() as stack:
        def sb(name, shape, dt=F32):
            return stack.enter_context(nc.sbuf_tensor(name, shape, dt))

        def bank(name):
            return stack.enter_context(nc.psum_tensor(name, [P, 512], F32))

        def sem(name):
            return stack.enter_context(nc.semaphore(name))

        ident = sb("ident", [P, P])
        neg_half, neg_one = sb("neg_half", [P, T]), sb("neg_one", [P, 1])
        ones = sb("ones", [P, P])
        wt_hi, wt_lo = sb("wt_hi", [P, DT, H], F32R), sb("wt_lo", [P, DT, H], F32R)
        wa_hi, wa_lo = sb("wa_hi", [P, CT, H], F32R), sb("wa_lo", [P, CT, H], F32R)
        wao_hi, wao_lo = sb("wao_hi", [P, CT, H], F32R), sb("wao_lo", [P, CT, H], F32R)
        bao_row = sb("bao_row", [P, H])
        go_row, betao_row = sb("go_row", [P, H]), sb("betao_row", [P, H])
        ba_col, bt_col = sb("ba_col", [P, HT]), sb("bt_col", [P, HT])
        bac_col, btc_col = sb("bac_col", [P, HT]), sb("btc_col", [P, HT])
        wa_mean, wt_mean = sb("wa_mean", [P, CT]), sb("wt_mean", [P, DT])
        b_sum, b_mean = sb("b_sum", [P, 2]), sb("b_mean", [P, 2])
        g1_col, beta1_col = sb("g1_col", [P, HT]), sb("beta1_col", [P, HT])
        g2_col, beta2_col = sb("g2_col", [P, HT]), sb("beta2_col", [P, HT])
        x_in, c_in = sb("x_in", [P, T, D]), sb("c_in", [P, T, DC])
        c_kept = sb("c_kept", [P, T, DC])
        c_hi, c_lo = sb("c_hi", [P, T, DC], F32R), sb("c_lo", [P, T, DC], F32R)
        y_rows = [sb(f"y_rows{n}", [P, T, H]) for n in range(2)]
        xT_hi, xT_lo = sb("xT_hi", [P, DT, T * P], F32R), sb("xT_lo", [P, DT, T * P], F32R)
        cT_hi, cT_lo = sb("cT_hi", [P, CT, T * P], F32R), sb("cT_lo", [P, CT, T * P], F32R)
        k_cols, q_cols = sb("k_cols", [P, HT, T * P]), sb("q_cols", [P, HT, T * P])
        squares, square_sum = sb("squares", [P, HT, T * P]), sb("square_sum", [P, T * P])
        kT_hi, kT_lo = sb("kT_hi", [P, HT, T * P], F32R), sb("kT_lo", [P, HT, T * P], F32R)
        qT_hi, qT_lo = sb("qT_hi", [P, HT, T * P], F32R), sb("qT_lo", [P, HT, T * P], F32R)
        probs = sb("probs", [P, T, S])
        pT_hi, pT_lo = sb("pT_hi", [P, NB, ST * L], F32R), sb("pT_lo", [P, NB, ST * L], F32R)
        pcT_hi, pcT_lo = sb("pcT_hi", [P, CT, T * P], F32R), sb("pcT_lo", [P, CT, T * P], F32R)
        k_ssq, q_ssq = sb("k_ssq", [P, T]), sb("q_ssq", [P, T])
        k_ve, q_ve = sb("k_ve", [P, T]), sb("q_ve", [P, T])
        k_rs, q_rs = sb("k_rs", [P, T]), sb("q_rs", [P, T])
        y_bn, y_mv = sb("y_bn", [P, T, 6]), sb("y_mv", [P, T, 2])
        y_sc = sb("y_sc", [P, T, 3])
        row_max, neg_max = sb("row_max", [P, T]), sb("neg_max", [P, T])
        row_sum, row_inv = sb("row_sum", [P, T]), sb("row_inv", [P, T])

        wide = [bank(f"wide{t}") for t in range(T)]
        turn = [bank(f"turn{n}") for n in range(2)]
        score = [bank(f"score{b}") for b in range(NB)]

        wa_stage, wt_stage, wo_stage, waT_stage = k_cols, q_cols, y_rows[1], squares

        wa_loaded, wo_loaded, wt_loaded = sem("wa_loaded"), sem("wo_loaded"), sem("wt_loaded")
        params_loaded = sem("params_loaded")
        x_loaded, c_loaded, c_copied = sem("x_loaded"), sem("c_loaded"), sem("c_copied")
        stored = [sem(f"stored{t}") for t in range(T)]
        passed = sem("passed")
        ident_zeroed, ident_made = sem("ident_zeroed"), sem("ident_made")
        wa_summed, wa_mean_made = sem("wa_summed"), sem("wa_mean_made")
        wa_hi_made, wa_split = sem("wa_hi_made"), sem("wa_split")
        wt_summed, wt_mean_made = sem("wt_summed"), sem("wt_mean_made")
        wt_hi_made, wt_split = sem("wt_hi_made"), sem("wt_split")
        b_spread, b_summed, b_mean_made, b_centred = (sem("b_spread"), sem("b_summed"), sem("b_mean_made"),
                                                      sem("b_centred"))
        waT_done, waT_copied = sem("waT_done"), sem("waT_copied")
        wao_done, wao_hi_made, wao_split = sem("wao_done"), sem("wao_hi_made"), sem("wao_split")
        bao_done, bao_made = sem("bao_done"), sem("bao_made")
        k_done, q_done, out_done = sem("k_done"), sem("q_done"), sem("out_done")
        xT_done, cT_done = sem("xT_done"), sem("cT_done")
        k_sum_turned, q_sum_turned, pT_done = sem("k_sum_turned"), sem("q_sum_turned"), sem("pT_done")
        k_rs_spread, q_rs_spread = sem("k_rs_spread"), sem("q_rs_spread")
        score_done, pc_done = sem("score_done"), sem("pc_done")
        xT_hi_made, cT_hi_made = sem("xT_hi_made"), sem("cT_hi_made")
        k_centred, k_squared = sem("k_centred"), sem("k_squared")
        q_centred, q_squared, y_normed = sem("q_centred"), sem("q_squared"), sem("y_normed")
        kT_hi_made, qT_hi_made = sem("kT_hi_made"), sem("qT_hi_made")
        probs_made, pT_hi_made, pc_hi_made = sem("probs_made"), sem("pT_hi_made"), sem("pc_hi_made")
        xT_split, cT_split, pT_split, pc_split = sem("xT_split"), sem("cT_split"), sem("pT_split"), sem("pc_split")
        k_added, k_summed, k_ssq_made = sem("k_added"), sem("k_summed"), sem("k_ssq_made")
        q_added, q_summed, q_ssq_made = sem("q_added"), sem("q_summed"), sem("q_ssq_made")
        k_normed, q_normed = sem("k_normed"), sem("q_normed")
        kT_split, qT_split = sem("kT_split"), sem("qT_split")
        y_summed, y_stats, y_moments = sem("y_summed"), sem("y_stats"), sem("y_moments")
        max_made, neg_max_made, sums_inverted = sem("max_made"), sem("neg_max_made"), sem("sums_inverted")
        k_paired, q_paired = sem("k_paired"), sem("q_paired")
        k_var, q_var, y_var = sem("k_var"), sem("q_var"), sem("y_var")
        k_rstd, q_rstd, y_rstd = sem("k_rstd"), sem("q_rstd"), sem("y_rstd")
        y_scales = sem("y_scales")
        c_hi_made, c_split, x_biased = sem("c_hi_made"), sem("c_split"), sem("x_biased")
        y_scaled, y_ready = sem("y_scaled"), sem("y_ready")

        def wait(eng, semaphore, value):
            if not isinstance(value, int) or value > 0:
                eng.wait_ge(semaphore, value)

        def wait_apart(eng, semaphore, value):
            if not isinstance(value, int) or value > 0:
                eng.wait_ge(semaphore, value)
                eng.sem_inc(passed, 1)

        def run_steps(eng, step):
            step(0, 0, first=True)
            step(1, 1)
            with eng.Fori(2, N - 2, 2) as i:
                step(i, 0)
                step(i + 1, 1)
            step(N - 2, 0)
            step(N - 1, 1, last=True)

        block = stack.enter_context(nc.Block())

        @block.sync
        def _(sp):
            def load_c(i):
                sp.dma_start(c_in[:], c_v[i]).then_inc(c_loaded, 16)

            def load_x(i, t):
                sp.dma_start(x_in[:, t, :], x_v[i, :, t, :]).then_inc(x_loaded, 16)

            sp.dma_start(wa_stage[:, 0:CT, :], w_audio.rearrange("(t p) h -> p t h", p=P)).then_inc(wa_loaded, 16)
            load_c(0)
            sp.dma_start(wo_stage[:], w_out.rearrange("(t p) h -> p t h", p=P)).then_inc(wo_loaded, 16)
            columns = [(ba_col, b_audio), (bt_col, b_text), (g1_col, g1), (beta1_col, beta1), (g2_col, g2), (beta2_col, beta2)]
            rows = [(bao_row, b_out), (go_row, g_out), (betao_row, beta_out)]
            for to, of in columns:
                sp.dma_start(to[:], of.rearrange("(t p) -> p t", p=P), allow_slow_non_contiguous=True).then_inc(params_loaded, 16)
            for to, of in rows:
                sp.dma_start(to[:], of.partition_broadcast(P)).then_inc(params_loaded, 16)
            sp.dma_start(wt_stage[:], w_text.rearrange("(t p) h -> p t h", p=P)).then_inc(wt_loaded, 16)
            for t in range(T):
                load_x(0, t)

            def store_y(j, odd, t):
                wait_apart(sp, y_ready, T * j + t + 1)
                sp.dma_start(out_v[j, :, t, :], y_rows[odd][:, t, :]).then_inc(stored[t], 16)

            def step(i, odd, first=False, last=False):
                if not isinstance(i, int) or i >= 2:
                    store_y(i - 2, odd, 2)
                    store_y(i - 2, odd, 3)
                if not first:
                    wait_apart(sp, c_split, T * i)
                wait_apart(sp, c_loaded, 16 * (i + 1))
                sp.dma_start(c_kept[:], c_in[:]).then_inc(c_copied, 16)
                if not last:
                    wait_apart(sp, c_copied, 16 * (i + 1))
                    wait_apart(sp, cT_done, CT * (i + 1))
                    load_c(i + 1)
                    wait_apart(sp, xT_done, DT * (i + 1))
                    for t in range(T):
                        wait_apart(sp, x_biased, T * i + t + 1)
                        load_x(i + 1, t)
                if not first:
                    store_y(i - 1, 1 - odd, 0)
                    store_y(i - 1, 1 - odd, 1)

            run_steps(sp, step)
            store_y(N - 2, 0, 2)
            store_y(N - 2, 0, 3)
            for t in range(T):
                store_y(N - 1, 1, t)
            for t in range(T):
                sp.wait_ge(stored[t], 16 * N)

        @block.tensor
        def _(pe):
            def product(to, terms, ready=None, count=0):
                n = len(terms)
                for m, (a_hi, a_lo, b_hi, b_lo) in enumerate(terms):
                    if ready is not None:
                        pe.wait_ge(ready, count + m + 1)
                    nc.tensor.matmul(to, a_hi, b_hi, start=(m == 0), stop=False)
                    nc.tensor.matmul(to, a_hi, b_lo, start=False, stop=False)
                    done = nc.tensor.matmul(to, a_lo, b_hi, start=False, stop=(m == n - 1))
                return done

            def transposes(to, blocks):
                for m, b in enumerate(blocks):
                    done = nc.tensor.transpose(to[:, m * P:(m + 1) * P], b, ident[:])
                return done

            def project_k(i, h):
                wait(pe, y_summed, T * (i - 2) + h + 1)
                cols = slice(h * P, (h + 1) * P)
                terms = [(wa_hi[:, d, cols], wa_lo[:, d, cols], cT_hi[:, d, :], cT_lo[:, d, :]) for d in range(CT)]
                product(wide[h][:], terms, cT_split if h == 0 else None, CT * i).then_inc(k_done, 1)

            def project_q(i, h):
                pe.wait_ge(k_centred, HT * i + h + 1)
                cols = slice(h * P, (h + 1) * P)
                terms = [(wt_hi[:, d, cols], wt_lo[:, d, cols], xT_hi[:, d, :], xT_lo[:, d, :]) for d in range(DT)]
                product(wide[h][:], terms, xT_split if h == 0 else None, DT * i).then_inc(q_done, 1)

            def turn_x(i, d):
                if d == 0:
                    pe.wait_ge(x_loaded, 16 * T * (i + 1))
                transposes(turn[d % 2], [x_in[:, t, d * P:(d + 1) * P] for t in range(T)]).then_inc(xT_done, 1)

            def turn_c(i, d):
                if d == 0:
                    pe.wait_ge(c_loaded, 16 * (i + 1))
                transposes(turn[d % 2], [c_in[:, t, d * P:(d + 1) * P] for t in range(T)]).then_inc(cT_done, 1)

            def turn_sum(i, to, summed, turned):
                pe.wait_ge(summed, i + 1)
                transposes(to, [square_sum[:, t * P:(t + 1) * P] for t in range(T)]).then_inc(turned, 1)

            def spread_rs(i, to, rs, rstd, spread):
                pe.wait_ge(rstd, i + 1)
                transposes(to, [rs[:, t:t + 1].broadcast_to([P, P]) for t in range(T)]).then_inc(spread, 1)

            def turn_p(j, b):
                pe.wait_ge(probs_made, T * j + LT * (b + 1))
                transposes(turn[b], [probs[:, LT * b + l, s * P:(s + 1) * P] for s in range(ST) for l in range(LT)]
                           ).then_inc(pT_done, 1)

            def scores(i, b, l):
                at = LT * b + l
                rows, keys = slice(at * P, (at + 1) * P), slice(b * S, (b + 1) * S)
                done = product(score[b][:, l * S:(l + 1) * S],
                               [(qT_hi[:, h, rows], qT_lo[:, h, rows], kT_hi[:, h, keys], kT_lo[:, h, keys])
                                for h in range(HT)], qT_split if at == 0 else None, HT * i)
                if l == LT - 1:
                    done.then_inc(score_done, 1)

            def probs_context(j, d):
                if d == 0:
                    pe.wait_ge(c_split, T * (j + 1))
                    pe.wait_ge(pT_split, NB * (j + 1))
                to = (score[0], score[1], turn[0])[d]
                cols = slice(d * P, (d + 1) * P)
                for b in range(NB):
                    done = product(to[:, b * L:(b + 1) * L],
                                   [(c_hi[:, ST * b + s, cols], c_lo[:, ST * b + s, cols],
                                     pT_hi[:, b, s * L:(s + 1) * L], pT_lo[:, b, s * L:(s + 1) * L])
                                    for s in range(ST)])
                done.then_inc(pc_done, 1)

            def output(j, t):
                rows = slice(t * P, (t + 1) * P)
                terms = [(pcT_hi[:, d, rows], pcT_lo[:, d, rows], wao_hi[:, d, :], wao_lo[:, d, :]) for d in range(CT)]
                product(wide[t][:], terms, pc_split if t == 0 else None, CT * j).then_inc(out_done, 1)

            pe.wait_ge(ident_made, 1)
            pe.wait_ge(wa_loaded, 16)
            for h in range(HT):
                transposes(wide[h], [wa_stage[:, d, h * P:(h + 1) * P] for d in range(CT)]).then_inc(waT_done, 1)
            turn_c(0, 0)
            turn_c(0, 1)
            pe.wait_ge(cT_split, 1)
            turn_c(0, 2)
            pe.wait_ge(waT_copied, HT)
            pe.wait_ge(wo_loaded, 16)
            for d in range(CT):
                for h in range(HT):
                    done = nc.tensor.matmul(wide[d][:], waT_stage[:, h, d * P:(d + 1) * P], wo_stage[:, h, :],
                                            start=(h == 0), stop=(h == HT - 1))
                done.then_inc(wao_done, 1)
            pe.wait_ge(params_loaded, 16 * 9)
            for h in range(HT):
                done = nc.tensor.matmul(wide[CT][:], ba_col[:, h:h + 1].broadcast_to([P, P]), wo_stage[:, h, :],
                                        start=(h == 0), stop=(h == HT - 1))
            done.then_inc(bao_done, 1)
            pe.wait_ge(ident_made, 2)
            nc.tensor.matmul(score[0][:, 0:HT], ones[:], ba_col[:], start=True, stop=True)
            nc.tensor.matmul(score[0][:, HT:2 * HT], ones[:], bt_col[:], start=True, stop=True).then_inc(b_spread, 1)
            pe.wait_ge(wa_split, CT)
            pe.wait_ge(wao_split, CT)
            pe.wait_ge(bao_made, 1)

            def step(i, odd, first=False, last=False):
                j = i - 1
                project_k(i, 0)
                if not first:
                    turn_p(j, 0)
                project_k(i, 1)
                if not first:
                    turn_p(j, 1)
                    pe.wait_ge(pT_split, NB * j + 1)
                turn_x(i, 0)
                project_k(i, 2)
                if not first:
                    pe.wait_ge(pT_split, NB * j + 2)
                turn_x(i, 1)
                pe.wait_ge(xT_split, DT * i + 1)
                turn_x(i, 2)
                project_k(i, 3)
                pe.wait_ge(xT_split, DT * i + 2)
                turn_x(i, 3)
                if first:
                    pe.wait_ge(wt_split, DT)
                project_q(i, 0)
                turn_sum(i, turn[0], k_summed, k_sum_turned)
                project_q(i, 1)
                spread_rs(i, turn[0], k_rs, k_rstd, k_rs_spread)
                project_q(i, 2)
                project_q(i, 3)
                if not first:
                    probs_context(j, 0)
                    probs_context(j, 1)
                turn_sum(i, turn[1], q_summed, q_sum_turned)
                if not first:
                    pe.wait_ge(k_normed, HT * (i + 1))
                    probs_context(j, 2)
                    pe.wait_ge(q_centred, HT * i + 1)
                    output(j, 0)
                spread_rs(i, turn[1], q_rs, q_rstd, q_rs_spread)
                if not first:
                    for t in range(1, T):
                        pe.wait_ge(q_centred, HT * i + t + 1)
                        output(j, t)
                if not last:
                    pe.wait_ge(k_normed, HT * (i + 1))
                    turn_c(i + 1, 0)
                    pe.wait_ge(q_normed, HT * (i + 1))
                    turn_c(i + 1, 1)
                pe.wait_ge(kT_split, HT * (i + 1))
                scores(i, 0, 0)
                if not last:
                    pe.wait_ge(cT_split, CT * (i + 1) + 1)
                    turn_c(i + 1, 2)
                scores(i, 0, 1)
                scores(i, 1, 0)
                scores(i, 1, 1)

            run_steps(pe, step)
            turn_p(N - 1, 0)
            turn_p(N - 1, 1)
            for d in range(CT):
                probs_context(N - 1, d)
            for t in range(T):
                output(N - 1, t)

        @block.scalar
        def _(act):
            def xT_high(i, d):
                act.wait_ge(xT_done, DT * i + d + 1)
                wait(act, q_done, T * i)
                nc.scalar.copy(xT_hi[:, d, :], turn[d % 2][:]).then_inc(xT_hi_made, 1)

            def cT_high(i, d):
                act.wait_ge(cT_done, CT * i + d + 1)
                wait(act, k_done, T * i)
                nc.scalar.copy(cT_hi[:, d, :], turn[d % 2][:]).then_inc(cT_hi_made, 1)

            def pT_high(j, b):
                act.wait_ge(pT_done, NB * j + b + 1)
                wait(act, pc_done, CT * j)
                nc.scalar.copy(pT_hi[:, b, :], turn[b][:]).then_inc(pT_hi_made, 1)

            def pc_high(j, d):
                act.wait_ge(pc_done, CT * j + d + 1)
                wait(act, out_done, T * j)
                of = (score[0], score[1], turn[0])[d]
                nc.scalar.copy(pcT_hi[:, d, :], of[:]).then_inc(pc_hi_made, 1)

            def centre(to, h, bias, done, i, centred, squared):
                act.wait_ge(done, HT * i + h + 1)
                nc.scalar.activation(squares[:, h, :], wide[h][:], ACT.Square, bias=bias[:, h:h + 1]).then_inc(squared, 1)
                nc.scalar.activation(to[:, h, :], wide[h][:], ACT.Identity, bias=bias[:, h:h + 1]).then_inc(centred, 1)

            def k_centre(i, h):
                wait(act, kT_split, HT * (i - 1) + h + 1)
                wait(act, q_summed, i)
                centre(k_cols, h, bac_col, k_done, i, k_centred, k_squared)

            def q_centre(i, h):
                wait(act, qT_split, HT * (i - 1) + h + 1)
                act.wait_ge(k_summed, i + 1)
                centre(q_cols, h, btc_col, q_done, i, q_centred, q_squared)

            def k_high(i, h):
                act.wait_ge(k_normed, HT * i + h + 1)
                nc.scalar.activation(kT_hi[:, h, :], k_cols[:, h, :], ACT.Identity,
                                     bias=beta2_col[:, h:h + 1]).then_inc(kT_hi_made, 1)

            def q_high(i, h):
                act.wait_ge(q_normed, HT * i + h + 1)
                nc.scalar.activation(qT_hi[:, h, :], q_cols[:, h, :], ACT.Identity,
                                     bias=beta1_col[:, h:h + 1]).then_inc(qT_hi_made, 1)

            def y_norm(j, odd, t):
                act.wait_ge(y_scales, T * j + t + 1)
                nc.scalar.activation(y_rows[odd][:, t, :], y_rows[odd][:, t, :], ACT.Identity,
                                     scale=y_sc[:, t, 0:1], bias=y_sc[:, t, 1:2]).then_inc(y_normed, 1)

            def exponentials(i, b):
                act.wait_ge(neg_max_made, NB * i + b + 1)
                wait(act, pT_done, NB * (i - 1) + b + 1)
                wait(act, sums_inverted, i)
                for l in range(LT):
                    at = LT * b + l
                    nc.scalar.activation(probs[:, at, :], score[b][:, l * S:(l + 1) * S], ACT.Exp,
                                         scale=SCALE, bias=neg_max[:, at:at + 1],
                                         accum_out=row_sum[:, at:at + 1]).then_inc(probs_made, 1)

            for h in range(HT):
                act.wait_ge(waT_done, h + 1)
                nc.scalar.copy(waT_stage[:, h, 0:DC], wide[h][:, 0:DC]).then_inc(waT_copied, 1)
            for d in range(CT):
                cT_high(0, d)
            for d in range(CT):
                act.wait_ge(wao_done, d + 1)
                nc.scalar.copy(wao_hi[:, d, :], wide[d][:]).then_inc(wao_hi_made, 1)
            act.wait_ge(params_loaded, 16 * 9)
            act.wait_ge(b_centred, 2)

            def step(i, odd, first=False, last=False):
                j = i - 1
                if not first:
                    pT_high(j, 0)
                k_centre(i, 0)
                k_centre(i, 1)
                if not first:
                    pT_high(j, 1)
                if not isinstance(i, int) or i >= 2:
                    y_norm(i - 2, odd, 2)
                xT_high(i, 0)
                if not isinstance(i, int) or i >= 2:
                    y_norm(i - 2, odd, 3)
                k_centre(i, 2)
                xT_high(i, 1)
                xT_high(i, 2)
                xT_high(i, 3)
                k_centre(i, 3)
                q_centre(i, 0)
                q_centre(i, 1)
                k_high(i, 0)
                k_high(i, 1)
                q_centre(i, 2)
                k_high(i, 2)
                k_high(i, 3)
                q_centre(i, 3)
                if not first:
                    for d in range(CT):
                        pc_high(j, d)
                for h in range(HT):
                    q_high(i, h)
                if not last:
                    cT_high(i + 1, 0)
                    cT_high(i + 1, 1)
                    cT_high(i + 1, 2)
                if not first:
                    y_norm(j, 1 - odd, 0)
                exponentials(i, 0)
                if not first:
                    y_norm(j, 1 - odd, 1)
                exponentials(i, 1)

            run_steps(act, step)
            y_norm(N - 2, 0, 2)
            y_norm(N - 2, 0, 3)
            for b in range(NB):
                pT_high(N - 1, b)
            for d in range(CT):
                pc_high(N - 1, d)
            for t in range(T):
                y_norm(N - 1, 1, t)

        @block.vector
        def _(dve):
            def low(to, whole, hi):
                return nc.vector.tensor_tensor(to, whole, hi.bitcast(F32), ALU.subtract)

            def xT_low(i, d):
                dve.wait_ge(xT_hi_made, DT * i + d + 1)
                low(xT_lo[:, d, :], turn[d % 2][:], xT_hi[:, d, :]).then_inc(xT_split, 1)

            def cT_low(i, d):
                dve.wait_ge(cT_hi_made, CT * i + d + 1)
                low(cT_lo[:, d, :], turn[d % 2][:], cT_hi[:, d, :]).then_inc(cT_split, 1)

            def pT_low(j, b):
                dve.wait_ge(pT_hi_made, NB * j + b + 1)
                low(pT_lo[:, b, :], turn[b][:], pT_hi[:, b, :]).then_inc(pT_split, 1)

            def pc_low(j, d):
                dve.wait_ge(pc_hi_made, CT * j + d + 1)
                of = (score[0], score[1], turn[0])[d]
                low(pcT_lo[:, d, :], of[:], pcT_hi[:, d, :]).then_inc(pc_split, 1)

            def add_square(i, paired, squared, added):
                dve.wait_ge(paired, i + 1)
                dve.wait_ge(squared, HT * i + 3)
                nc.vector.tensor_tensor(squares[:, 2, :], squares[:, 0, :], squares[:, 2, :],
                                        ALU.add).then_inc(added, 1)

            def sum_squares(i, squared, added, summed, sum_turned, before):
                wait(dve, sum_turned, before)
                dve.wait_ge(added, i + 1)
                dve.wait_ge(squared, HT * (i + 1))
                nc.vector.tensor_tensor(square_sum[:], squares[:, 2, :], squares[:, 3, :],
                                        ALU.add).then_inc(summed, 1)

            def sum_rows(i, of, turned, ssq, made):
                dve.wait_ge(turned, i + 1)
                nc.vector.reduce_sum(ssq[:], of[:].rearrange("p (t f) -> p t f", t=T), AX_X).then_inc(made, 1)

            def norm(i, h, rs, cols, gain, centred, spread, normed):
                if h == 0:
                    dve.wait_ge(spread, i + 1)
                dve.wait_ge(centred, HT * i + h + 1)
                nc.vector.scalar_tensor_tensor(out=cols[:, h, :], in0=cols[:, h, :], scalar=gain[:, h:h + 1],
                                               in1=rs[:], op0=ALU.mult, op1=ALU.mult).then_inc(normed, 1)

            def shifted_low(i, h, lo, hi, cols, shift, hi_made, split):
                dve.wait_ge(hi_made, HT * i + h + 1)
                nc.vector.scalar_tensor_tensor(out=lo[:, h, :], in0=cols[:, h, :], scalar=shift[:, h:h + 1],
                                               in1=hi[:, h, :].bitcast(F32), op0=ALU.add,
                                               op1=ALU.subtract).then_inc(split, 1)

            def k_norm(i, h):
                norm(i, h, turn[0], k_cols, g2_col, k_centred, k_rs_spread, k_normed)

            def q_norm(i, h):
                norm(i, h, turn[1], q_cols, g1_col, q_centred, q_rs_spread, q_normed)

            def k_low(i, h):
                shifted_low(i, h, kT_lo, kT_hi, k_cols, beta2_col, kT_hi_made, kT_split)

            def q_low(i, h):
                shifted_low(i, h, qT_lo, qT_hi, q_cols, beta1_col, qT_hi_made, qT_split)

            def y_sum(j, odd, t):
                dve.wait_ge(out_done, T * j + t + 1)
                dve.wait_ge(x_biased, T * j + t + 1)
                dve.wait_ge(sums_inverted, j + 1)
                rows = y_rows[odd][:, t, :]
                nc.vector.scalar_tensor_tensor(out=rows, in0=wide[t][:], scalar=row_inv[:, t:t + 1],
                                               in1=rows, op0=ALU.mult, op1=ALU.add).then_inc(y_summed, 1)

            def y_stat(j, odd, t):
                dve.wait_ge(y_summed, T * j + t + 1)
                nc.vector.bn_stats(y_bn[:, t, :], y_rows[odd][:, t, :]).then_inc(y_stats, 1)

            def y_moment(j, t):
                wait_apart(dve, y_stats, T * j + t + 1)
                nc.vector.bn_aggr(y_mv[:, t, :], y_bn[:, t, :]).then_inc(y_moments, 1)

            def maxima(i, b):
                tiles = slice(LT * b, LT * (b + 1))
                dve.wait_ge(score_done, NB * i + b + 1)
                nc.vector.reduce_max(row_max[:, tiles], score[b][:].rearrange("p (l s) -> p l s", l=LT),
                                     AX_X).then_inc(max_made, 1)
                dve.wait_ge(max_made, NB * i + b + 1)
                nc.vector.tensor_scalar(neg_max[:, tiles], row_max[:, tiles], -SCALE, None,
                                        ALU.mult).then_inc(neg_max_made, 1)

            def invert_sums(j):
                dve.wait_ge(probs_made, T * (j + 1))
                nc.vector.reciprocal(row_inv[:], row_sum[:]).then_inc(sums_inverted, 1)

            def split_weights(to_hi, to_lo, of, n, mean, summed, mean_made, hi_made, split):
                nc.vector.reduce_sum(mean[:], of[:, 0:n, :], AX_X).then_inc(summed, 1)
                dve.wait_ge(summed, 1)
                nc.vector.tensor_scalar(mean[:], mean[:], -1.0 / H, None, ALU.mult).then_inc(mean_made, 1)
                dve.wait_ge(mean_made, 1)
                for d in range(n):
                    nc.vector.tensor_scalar(to_hi[:, d, :], of[:, d, :], mean[:, d:d + 1], None,
                                            ALU.add).then_inc(hi_made, 1)
                for d in range(n):
                    dve.wait_ge(hi_made, d + 1)
                    nc.vector.scalar_tensor_tensor(out=to_lo[:, d, :], in0=of[:, d, :], scalar=mean[:, d:d + 1],
                                                   in1=to_hi[:, d, :].bitcast(F32), op0=ALU.add,
                                                   op1=ALU.subtract).then_inc(split, 1)

            dve.wait_ge(wa_loaded, 16)
            split_weights(wa_hi, wa_lo, wa_stage, CT, wa_mean, wa_summed, wa_mean_made, wa_hi_made, wa_split)
            for d in range(CT):
                cT_low(0, d)
            dve.wait_ge(wt_loaded, 16)
            split_weights(wt_hi, wt_lo, wt_stage, DT, wt_mean, wt_summed, wt_mean_made, wt_hi_made, wt_split)
            for d in range(CT):
                dve.wait_ge(wao_hi_made, d + 1)
                low(wao_lo[:, d, :], wide[d][:], wao_hi[:, d, :]).then_inc(wao_split, 1)
            dve.wait_ge(bao_done, 1)
            dve.wait_ge(params_loaded, 16 * 9)
            nc.vector.tensor_tensor(bao_row[:], wide[CT][:], bao_row[:], ALU.add).then_inc(bao_made, 1)
            dve.wait_ge(b_spread, 1)
            nc.vector.reduce_sum(b_sum[:], score[0][:, 0:2 * HT].rearrange("p (n h) -> p n h", n=2),
                                 AX_X).then_inc(b_summed, 1)
            dve.wait_ge(b_summed, 1)
            nc.vector.tensor_scalar(b_mean[:], b_sum[:], -1.0 / H, None, ALU.mult).then_inc(b_mean_made, 1)
            dve.wait_ge(b_mean_made, 1)
            for n, (to, of) in enumerate(((bac_col, ba_col), (btc_col, bt_col))):
                nc.vector.tensor_scalar(to[:], of[:], b_mean[:, n:n + 1], None, ALU.add).then_inc(b_centred, 1)

            def step(i, odd, first=False, last=False):
                j = i - 1
                if not first:
                    invert_sums(j)
                    pT_low(j, 0)
                    pT_low(j, 1)
                xT_low(i, 0)
                xT_low(i, 1)
                xT_low(i, 2)
                add_square(i, k_paired, k_squared, k_added)
                xT_low(i, 3)
                sum_squares(i, k_squared, k_added, k_summed, q_sum_turned, i)
                sum_rows(i, turn[0], k_sum_turned, k_ssq, k_ssq_made)
                k_norm(i, 0)
                k_norm(i, 1)
                k_low(i, 0)
                k_norm(i, 2)
                k_norm(i, 3)
                k_low(i, 1)
                add_square(i, q_paired, q_squared, q_added)
                k_low(i, 2)
                sum_squares(i, q_squared, q_added, q_summed, k_sum_turned, i + 1)
                k_low(i, 3)
                if not first:
                    pc_low(j, 0)
                sum_rows(i, turn[1], q_sum_turned, q_ssq, q_ssq_made)
                if not first:
                    pc_low(j, 1)
                    pc_low(j, 2)
                q_norm(i, 0)
                q_norm(i, 1)
                q_low(i, 0)
                q_norm(i, 2)
                q_low(i, 1)
                q_norm(i, 3)
                q_low(i, 2)
                q_low(i, 3)
                if not first:
                    y_sum(j, 1 - odd, 0)
                    y_sum(j, 1 - odd, 1)
                if not last:
                    cT_low(i + 1, 0)
                if not first:
                    y_stat(j, 1 - odd, 0)
                    y_stat(j, 1 - odd, 1)
                    y_moment(j, 0)
                if not last:
                    cT_low(i + 1, 1)
                if not first:
                    y_moment(j, 1)
                    y_sum(j, 1 - odd, 2)
                    y_sum(j, 1 - odd, 3)
                if not last:
                    cT_low(i + 1, 2)
                maxima(i, 0)
                if not first:
                    y_stat(j, 1 - odd, 2)
                    y_stat(j, 1 - odd, 3)
                maxima(i, 1)
                if not first:
                    y_moment(j, 2)
                    y_moment(j, 3)

            run_steps(dve, step)
            invert_sums(N - 1)
            for b in range(NB):
                pT_low(N - 1, b)
            for d in range(CT):
                pc_low(N - 1, d)
            for t in range(T):
                y_sum(N - 1, 1, t)
                y_stat(N - 1, 1, t)
                y_moment(N - 1, t)

        @block.gpsimd
        def _(pool):
            def scales(i, t, moments, mv, sc, var, rstd, made):
                at = T * i + t + 1
                wait_apart(pool, moments, at)
                nc.gpsimd.tensor_scalar(sc[:, t, 2:3], mv[:, t, 1:2], EPS, 1.0, ALU.add, ALU.mult).then_inc(var, 1)
                pool.wait_ge(var, at)
                nc.gpsimd.tensor_tensor(sc[:, t, 0:1], sc[:, t, 2:3], neg_half[:, 0:1], ALU.pow).then_inc(rstd, 1)
                wait_apart(pool, rstd, at)
                nc.gpsimd.tensor_scalar(sc[:, t, 1:2], mv[:, t, 0:1], sc[:, t, 0:1], neg_one[:, 0:1],
                                        ALU.mult, ALU.mult).then_inc(made, 1)

            def pair_squares(i, squared, paired):
                pool.wait_ge(squared, HT * i + 2)
                nc.gpsimd.tensor_tensor(squares[:, 0, :], squares[:, 0, :], squares[:, 1, :],
                                        ALU.add).then_inc(paired, 1)

            def row_rstd(i, ssq_made, ssq, ve, rs, var, rstd):
                wait_apart(pool, ssq_made, i + 1)
                nc.gpsimd.tensor_scalar(ve[:], ssq[:], 1.0 / H, EPS, ALU.mult, ALU.add).then_inc(var, 1)
                pool.wait_ge(var, i + 1)
                nc.gpsimd.tensor_tensor(rs[:], ve[:], neg_half[:], ALU.pow).then_inc(rstd, 1)

            def y_scale(j, t):
                scales(j, t, y_moments, y_mv, y_sc, y_var, y_rstd, y_scales)

            def split_c(i, t):
                if t == 0:
                    wait_apart(pool, c_copied, 16 * (i + 1))
                    wait_apart(pool, pc_done, CT * i)
                nc.gpsimd.tensor_scalar(c_hi[:, t, :], c_kept[:, t, :], 1.0, 1.0, ALU.mult,
                                        ALU.mult).then_inc(c_hi_made, 1)
                pool.wait_ge(c_hi_made, T * i + t + 1)
                nc.gpsimd.tensor_tensor(c_lo[:, t, :], c_kept[:, t, :], c_hi[:, t, :].bitcast(F32),
                                        ALU.subtract).then_inc(c_split, 1)

            def bias_x(i, odd, t):
                if t == 0:
                    pool.wait_ge(x_loaded, 16 * T * (i + 1))
                wait(pool, stored[t], 16 * (i - 1))
                nc.gpsimd.tensor_tensor(y_rows[odd][:, t, :], x_in[:, t, :], bao_row[:], ALU.add).then_inc(x_biased, 1)

            def finish_y(j, odd, t):
                rows = y_rows[odd][:, t, :]
                pool.wait_ge(y_normed, T * j + t + 1)
                nc.gpsimd.tensor_tensor(rows, rows, go_row[:], ALU.mult).then_inc(y_scaled, 1)
                pool.wait_ge(y_scaled, T * j + t + 1)
                nc.gpsimd.tensor_tensor(rows, rows, betao_row[:], ALU.add).then_inc(y_ready, 1)

            nc.gpsimd.memset(ident[:], 0.0).then_inc(ident_zeroed, 1)
            nc.gpsimd.memset(neg_half[:], -0.5).then_inc(ident_zeroed, 1)
            nc.gpsimd.memset(neg_one[:], -1.0).then_inc(ident_zeroed, 1)
            pool.wait_ge(ident_zeroed, 3)
            nc.gpsimd.affine_select(out=ident[:], in_=ident[:], compare_op=ALU.not_equal, fill=1.0, base=0,
                                    pattern=[[-1, P]], channel_multiplier=1).then_inc(ident_made, 1)
            nc.gpsimd.memset(ones[:], 1.0).then_inc(ident_made, 1)

            def step(i, odd, first=False, last=False):
                j = i - 1
                if not isinstance(i, int) or i >= 2:
                    finish_y(i - 2, odd, 2)
                pair_squares(i, k_squared, k_paired)
                if not isinstance(i, int) or i >= 2:
                    finish_y(i - 2, odd, 3)
                if not first:
                    split_c(j, 0)
                row_rstd(i, k_ssq_made, k_ssq, k_ve, k_rs, k_var, k_rstd)
                if not first:
                    split_c(j, 1)
                pair_squares(i, q_squared, q_paired)
                if not first:
                    split_c(j, 2)
                    split_c(j, 3)
                row_rstd(i, q_ssq_made, q_ssq, q_ve, q_rs, q_var, q_rstd)
                if first:
                    pool.wait_ge(bao_made, 1)
                for t in range(T):
                    bias_x(i, odd, t)
                if not first:
                    y_scale(j, 0)
                    y_scale(j, 1)
                    finish_y(j, 1 - odd, 0)
                    y_scale(j, 2)
                    y_scale(j, 3)
                    finish_y(j, 1 - odd, 1)

            run_steps(pool, step)
            for t in (2, 3):
                finish_y(N - 2, 0, t)
            for t in range(T):
                split_c(N - 1, t)
            for t in range(T):
                y_scale(N - 1, t)
                finish_y(N - 1, 1, t)


_INS = ["x", "ctx_768", "L0_xattn_W_text", "L0_xattn_b_text", "L0_xattn_W_audio", "L0_xattn_b_audio",
        "L0_xattn_W_out", "L0_xattn_b_out", "L0_xattn_g1", "L0_xattn_beta1", "L0_xattn_g2", "L0_xattn_beta2",
        "L0_xattn_g_out", "L0_xattn_beta_out"]


def kernel(**inputs):
    import numpy as _np
    import concourse.bacc as _bacc
    from concourse import mybir as _mybir
    from concourse.bass_utils import run_bass_kernel_spmd as _run

    nc = _bacc.Bacc("TRN2", target_bir_lowering=False, num_devices=1)
    arrays, args = {}, []
    for name in _INS:
        a = _np.ascontiguousarray(inputs[name])
        arrays[f"in_{name}"] = a
        args.append(nc.dram_tensor(f"in_{name}", a.shape, _mybir.dt.from_np(a.dtype), kind="ExternalInput").ap())
    out = nc.dram_tensor("out", arrays["in_x"].shape, _mybir.dt.float32, kind="ExternalOutput").ap()
    cross_attention_kernel(nc, *args, out)
    r = _run(nc, [arrays], core_ids=[0])
    return r.results[0]["out"]
```

```python
from contextlib import ExitStack

import numpy as np

import concourse.bass as bass
from concourse import mybir

F32 = mybir.dt.float32
F32R = mybir.dt.float32r
ALU = mybir.AluOpType
ACT = mybir.ActivationFunctionType
AX_X = mybir.AxisListType.X

P = 128
EPS = 1e-5


def cross_attention_kernel(nc, x, ctx, w_text, b_text, w_audio, b_audio, w_out, b_out,
                           g1, beta1, g2, beta2, g_out, beta_out, out):
    B, L, D = x.shape
    S, DC = ctx.shape[1], ctx.shape[2]
    H = w_text.shape[1]
    NB = 2
    N = B // NB
    DT, CT, HT = D // P, DC // P, H // P
    LT, ST = L // P, S // P
    T = NB * LT
    assert D == H == 4 * P and LT == ST == 2 and T == HT == DT and NB * L == 512 and N >= 6 and N % 2 == 0
    SCALE = float(1.0 / np.sqrt(np.float32(H)))

    x_v = x.rearrange("(i b) (t p) d -> i p (b t) d", b=NB, p=P)
    c_v = ctx.rearrange("(i b) (t p) d -> i p (b t) d", b=NB, p=P)
    out_v = out.rearrange("(i b) (t p) d -> i p (b t) d", b=NB, p=P)

    with ExitStack() as stack:
        def sb(name, shape, dt=F32):
            return stack.enter_context(nc.sbuf_tensor(name, shape, dt))

        def bank(name):
            return stack.enter_context(nc.psum_tensor(name, [P, 512], F32))

        def sem(name):
            return stack.enter_context(nc.semaphore(name))

        ident = sb("ident", [P, P])
        neg_half, neg_one = sb("neg_half", [P, T]), sb("neg_one", [P, 1])
        ones = sb("ones", [P, P])
        wt_hi, wt_lo = sb("wt_hi", [P, DT, H], F32R), sb("wt_lo", [P, DT, H], F32R)
        wa_hi, wa_lo = sb("wa_hi", [P, CT, H], F32R), sb("wa_lo", [P, CT, H], F32R)
        wao_hi, wao_lo = sb("wao_hi", [P, CT, H], F32R), sb("wao_lo", [P, CT, H], F32R)
        bao_row = sb("bao_row", [P, H])
        go_row, betao_row = sb("go_row", [P, H]), sb("betao_row", [P, H])
        ba_col, bt_col = sb("ba_col", [P, HT]), sb("bt_col", [P, HT])
        bac_col, btc_col = sb("bac_col", [P, HT]), sb("btc_col", [P, HT])
        wa_mean, wt_mean = sb("wa_mean", [P, CT]), sb("wt_mean", [P, DT])
        b_sum, b_mean = sb("b_sum", [P, 2]), sb("b_mean", [P, 2])
        g1_col, beta1_col = sb("g1_col", [P, HT]), sb("beta1_col", [P, HT])
        g2_col, beta2_col = sb("g2_col", [P, HT]), sb("beta2_col", [P, HT])
        x_in, c_in = sb("x_in", [P, T, D]), sb("c_in", [P, T, DC])
        c_kept = sb("c_kept", [P, T, DC])
        c_hi, c_lo = sb("c_hi", [P, T, DC], F32R), sb("c_lo", [P, T, DC], F32R)
        y_rows = [sb(f"y_rows{n}", [P, T, H]) for n in range(2)]
        xT_hi, xT_lo = sb("xT_hi", [P, DT, T * P], F32R), sb("xT_lo", [P, DT, T * P], F32R)
        cT_hi, cT_lo = sb("cT_hi", [P, CT, T * P], F32R), sb("cT_lo", [P, CT, T * P], F32R)
        k_cols, q_cols = sb("k_cols", [P, HT, T * P]), sb("q_cols", [P, HT, T * P])
        squares, square_sum = sb("squares", [P, HT, T * P]), sb("square_sum", [P, T * P])
        kT_hi, kT_lo = sb("kT_hi", [P, HT, T * P], F32R), sb("kT_lo", [P, HT, T * P], F32R)
        qT_hi, qT_lo = sb("qT_hi", [P, HT, T * P], F32R), sb("qT_lo", [P, HT, T * P], F32R)
        probs = sb("probs", [P, T, S])
        pT_hi, pT_lo = sb("pT_hi", [P, NB, ST * L], F32R), sb("pT_lo", [P, NB, ST * L], F32R)
        pcT_hi, pcT_lo = sb("pcT_hi", [P, CT, T * P], F32R), sb("pcT_lo", [P, CT, T * P], F32R)
        k_ssq, q_ssq = sb("k_ssq", [P, T]), sb("q_ssq", [P, T])
        k_ve, q_ve = sb("k_ve", [P, T]), sb("q_ve", [P, T])
        k_rs, q_rs = sb("k_rs", [P, T]), sb("q_rs", [P, T])
        y_bn, y_mv = sb("y_bn", [P, T, 6]), sb("y_mv", [P, T, 2])
        y_sc = sb("y_sc", [P, T, 3])
        row_max, neg_max = sb("row_max", [P, T]), sb("neg_max", [P, T])
        row_sum, row_inv = sb("row_sum", [P, T]), sb("row_inv", [P, T])

        wide = [bank(f"wide{t}") for t in range(T)]
        turn = [bank(f"turn{n}") for n in range(2)]
        score = [bank(f"score{b}") for b in range(NB)]

        wa_stage, wt_stage, wo_stage, waT_stage = k_cols, q_cols, y_rows[1], y_rows[0]

        wa_loaded, wo_loaded, wt_loaded = sem("wa_loaded"), sem("wo_loaded"), sem("wt_loaded")
        columns_loaded, rows_loaded = sem("columns_loaded"), sem("rows_loaded")
        x_loaded, c_loaded, c_copied = sem("x_loaded"), sem("c_loaded"), sem("c_copied")
        stored = [sem(f"stored{t}") for t in range(T)]
        passed = sem("passed")
        ident_zeroed, ident_made = sem("ident_zeroed"), sem("ident_made")
        wa_summed, wa_mean_made = sem("wa_summed"), sem("wa_mean_made")
        wa_hi_made, wa_split = sem("wa_hi_made"), sem("wa_split")
        wt_summed, wt_mean_made = sem("wt_summed"), sem("wt_mean_made")
        wt_hi_made, wt_split = sem("wt_hi_made"), sem("wt_split")
        b_spread, b_summed, b_mean_made, b_centred = (sem("b_spread"), sem("b_summed"), sem("b_mean_made"),
                                                      sem("b_centred"))
        waT_done, waT_copied = sem("waT_done"), sem("waT_copied")
        wao_done, wao_hi_made, wao_split = sem("wao_done"), sem("wao_hi_made"), sem("wao_split")
        bao_done, bao_made = sem("bao_done"), sem("bao_made")
        k_done, q_done, out_done = sem("k_done"), sem("q_done"), sem("out_done")
        xT_done, cT_done = sem("xT_done"), sem("cT_done")
        k_sum_turned, q_sum_turned, pT_done = sem("k_sum_turned"), sem("q_sum_turned"), sem("pT_done")
        k_rs_spread, q_rs_spread = sem("k_rs_spread"), sem("q_rs_spread")
        score_done, pc_done = sem("score_done"), sem("pc_done")
        xT_hi_made, cT_hi_made = sem("xT_hi_made"), sem("cT_hi_made")
        k_centred, k_squared = sem("k_centred"), sem("k_squared")
        q_centred, q_squared, y_normed = sem("q_centred"), sem("q_squared"), sem("y_normed")
        kT_hi_made, qT_hi_made = sem("kT_hi_made"), sem("qT_hi_made")
        probs_made, pT_hi_made, pc_hi_made = sem("probs_made"), sem("pT_hi_made"), sem("pc_hi_made")
        xT_split, cT_split, pT_split, pc_split = sem("xT_split"), sem("cT_split"), sem("pT_split"), sem("pc_split")
        k_added, k_summed, k_ssq_made = sem("k_added"), sem("k_summed"), sem("k_ssq_made")
        q_added, q_summed, q_ssq_made = sem("q_added"), sem("q_summed"), sem("q_ssq_made")
        k_normed, q_normed = sem("k_normed"), sem("q_normed")
        kT_split, qT_split = sem("kT_split"), sem("qT_split")
        y_summed, y_stats, y_moments = sem("y_summed"), sem("y_stats"), sem("y_moments")
        max_made, neg_max_made, sums_inverted = sem("max_made"), sem("neg_max_made"), sem("sums_inverted")
        k_paired, q_paired = sem("k_paired"), sem("q_paired")
        k_var, q_var, y_var = sem("k_var"), sem("q_var"), sem("y_var")
        k_rstd, q_rstd, y_rstd = sem("k_rstd"), sem("q_rstd"), sem("y_rstd")
        y_scales = sem("y_scales")
        c_hi_made, c_split, x_biased = sem("c_hi_made"), sem("c_split"), sem("x_biased")
        y_scaled, y_ready = sem("y_scaled"), sem("y_ready")
        last_scaled = [sem("last_scaled_pool"), sem("last_scaled_dve")]
        last_ready = [sem("last_ready_pool"), sem("last_ready_dve")]

        def wait(eng, semaphore, value):
            if not isinstance(value, int) or value > 0:
                eng.wait_ge(semaphore, value)

        def wait_apart(eng, semaphore, value):
            if not isinstance(value, int) or value > 0:
                eng.wait_ge(semaphore, value)
                eng.sem_inc(passed, 1)

        def run_steps(eng, step):
            step(0, 0, first=True)
            step(1, 1)
            with eng.Fori(2, N - 2, 2) as i:
                step(i, 0)
                step(i + 1, 1)
            step(N - 2, 0)
            step(N - 1, 1, last=True)

        block = stack.enter_context(nc.Block())

        @block.sync
        def _(sp):
            def load_c(i):
                sp.dma_start(c_in[:], c_v[i]).then_inc(c_loaded, 16)

            def load_x(i, t):
                sp.dma_start(x_in[:, t, :], x_v[i, :, t, :]).then_inc(x_loaded, 16)

            sp.dma_start(wa_stage[:, 0:CT, :], w_audio.rearrange("(t p) h -> p t h", p=P)).then_inc(wa_loaded, 16)
            load_c(0)
            columns = [(ba_col, b_audio), (bt_col, b_text), (g1_col, g1), (beta1_col, beta1),
                       (g2_col, g2), (beta2_col, beta2)]
            rows = [(bao_row, b_out), (go_row, g_out), (betao_row, beta_out)]
            for to, of in columns:
                sp.dma_start(to[:], of.rearrange("(t p) -> p t", p=P),
                             allow_slow_non_contiguous=True).then_inc(columns_loaded, 16)
            sp.dma_start(wt_stage[:], w_text.rearrange("(t p) h -> p t h", p=P)).then_inc(wt_loaded, 16)
            for t in range(T):
                load_x(0, t)
            sp.dma_start(wo_stage[:], w_out.rearrange("(t p) h -> p t h", p=P)).then_inc(wo_loaded, 16)
            for to, of in rows:
                sp.dma_start(to[:], of.partition_broadcast(P)).then_inc(rows_loaded, 16)

            def store_y(j, odd, t):
                wait_apart(sp, y_ready, T * j + t + 1)
                sp.dma_start(out_v[j, :, t, :], y_rows[odd][:, t, :]).then_inc(stored[t], 16)

            def step(i, odd, first=False, last=False):
                if not isinstance(i, int) or i >= 2:
                    store_y(i - 2, odd, 2)
                    store_y(i - 2, odd, 3)
                if not first:
                    wait_apart(sp, c_split, T * i)
                wait_apart(sp, c_loaded, 16 * (i + 1))
                sp.dma_start(c_kept[:], c_in[:]).then_inc(c_copied, 16)
                if not last:
                    wait_apart(sp, c_copied, 16 * (i + 1))
                    wait_apart(sp, cT_done, CT * (i + 1))
                    load_c(i + 1)
                    wait_apart(sp, xT_done, DT * (i + 1))
                    for t in range(T):
                        wait_apart(sp, x_biased, T * i + t + 1)
                        load_x(i + 1, t)
                if not first:
                    store_y(i - 1, 1 - odd, 0)
                    store_y(i - 1, 1 - odd, 1)

            run_steps(sp, step)
            store_y(N - 2, 0, 2)
            store_y(N - 2, 0, 3)
            for t, by, count in ((0, 1, 1), (2, 1, 2), (1, 0, 1), (3, 1, 3)):
                sp.wait_ge(last_ready[by], count)
                sp.dma_start(out_v[N - 1, :, t, :], y_rows[1][:, t, :]).then_inc(stored[t], 16)
            for t in range(T):
                sp.wait_ge(stored[t], 16 * N)

        @block.tensor
        def _(pe):
            def product(to, terms, ready=None, count=0):
                n = len(terms)
                for m, (a_hi, a_lo, b_hi, b_lo) in enumerate(terms):
                    if ready is not None:
                        pe.wait_ge(ready, count + m + 1)
                    nc.tensor.matmul(to, a_hi, b_hi, start=(m == 0), stop=False)
                    nc.tensor.matmul(to, a_hi, b_lo, start=False, stop=False)
                    done = nc.tensor.matmul(to, a_lo, b_hi, start=False, stop=(m == n - 1))
                return done

            def transposes(to, blocks):
                for m, b in enumerate(blocks):
                    done = nc.tensor.transpose(to[:, m * P:(m + 1) * P], b, ident[:])
                return done

            def project_k(i, h):
                if isinstance(i, int) and i == 0:
                    pe.wait_ge(waT_copied, h + 1)
                wait(pe, y_summed, T * (i - 2) + h + 1)
                cols = slice(h * P, (h + 1) * P)
                terms = [(wa_hi[:, d, cols], wa_lo[:, d, cols], cT_hi[:, d, :], cT_lo[:, d, :]) for d in range(CT)]
                product(wide[h][:], terms, cT_split if h == 0 else None, CT * i).then_inc(k_done, 1)

            def project_q(i, h):
                pe.wait_ge(k_centred, HT * i + h + 1)
                cols = slice(h * P, (h + 1) * P)
                terms = [(wt_hi[:, d, cols], wt_lo[:, d, cols], xT_hi[:, d, :], xT_lo[:, d, :]) for d in range(DT)]
                product(wide[h][:], terms, xT_split if h == 0 else None, DT * i).then_inc(q_done, 1)

            def turn_x(i, d):
                if d == 0:
                    pe.wait_ge(x_loaded, 16 * T * (i + 1))
                transposes(turn[d % 2], [x_in[:, t, d * P:(d + 1) * P] for t in range(T)]).then_inc(xT_done, 1)

            def turn_c(i, d):
                to = score[1] if d == 2 and isinstance(i, int) and i == 0 else turn[d % 2]
                if d == 0:
                    pe.wait_ge(c_loaded, 16 * (i + 1))
                transposes(to, [c_in[:, t, d * P:(d + 1) * P] for t in range(T)]).then_inc(cT_done, 1)

            def turn_sum(i, to, summed, turned):
                pe.wait_ge(summed, i + 1)
                transposes(to, [square_sum[:, t * P:(t + 1) * P] for t in range(T)]).then_inc(turned, 1)

            def spread_rs(i, to, rs, rstd, spread):
                pe.wait_ge(rstd, i + 1)
                transposes(to, [rs[:, t:t + 1].broadcast_to([P, P]) for t in range(T)]).then_inc(spread, 1)

            def turn_p(j, b):
                pe.wait_ge(probs_made, T * j + LT * (b + 1))
                transposes(turn[b], [probs[:, LT * b + l, s * P:(s + 1) * P] for s in range(ST) for l in range(LT)]
                           ).then_inc(pT_done, 1)

            def scores(i, b, l):
                at = LT * b + l
                rows, keys = slice(at * P, (at + 1) * P), slice(b * S, (b + 1) * S)
                done = product(score[b][:, l * S:(l + 1) * S],
                               [(qT_hi[:, h, rows], qT_lo[:, h, rows], kT_hi[:, h, keys], kT_lo[:, h, keys])
                                for h in range(HT)], qT_split if at == 0 else None, HT * i)
                if l == LT - 1:
                    done.then_inc(score_done, 1)

            def probs_context(j, d, batches=range(NB)):
                if d == 0:
                    pe.wait_ge(c_split, T * (j + 1))
                    pe.wait_ge(pT_split, NB * j + batches[-1] + 1)
                to = (score[0], score[1], turn[0])[d]
                cols = slice(d * P, (d + 1) * P)
                for b in batches:
                    done = product(to[:, b * L:(b + 1) * L],
                                   [(c_hi[:, ST * b + s, cols], c_lo[:, ST * b + s, cols],
                                     pT_hi[:, b, s * L:(s + 1) * L], pT_lo[:, b, s * L:(s + 1) * L])
                                    for s in range(ST)])
                if batches[-1] == NB - 1:
                    done.then_inc(pc_done, 1)

            def output_part(j, t, d):
                pe.wait_ge(pc_split, CT * j + d + 1)
                rows = slice(t * P, (t + 1) * P)
                hi, lo = pcT_hi[:, d, rows], pcT_lo[:, d, rows]
                nc.tensor.matmul(wide[t][:], hi, wao_hi[:, d, :], start=(d == 0), stop=False)
                nc.tensor.matmul(wide[t][:], hi, wao_lo[:, d, :], start=False, stop=False)
                done = nc.tensor.matmul(wide[t][:], lo, wao_hi[:, d, :], start=False, stop=(d == CT - 1))
                if d == CT - 1:
                    done.then_inc(out_done, 1)

            def output(j, t):
                for d in range(CT):
                    output_part(j, t, d)

            def fold_weights(d):
                if d == 0:
                    pe.wait_ge(waT_copied, HT)
                    pe.wait_ge(wo_loaded, 16)
                pe.wait_ge(q_centred, d + 1)
                for h in range(HT):
                    done = nc.tensor.matmul(wide[d][:], waT_stage[:, h, d * P:(d + 1) * P], wo_stage[:, h, :],
                                            start=(h == 0), stop=(h == HT - 1))
                done.then_inc(wao_done, 1)

            def fold_bias():
                pe.wait_ge(q_centred, HT)
                for h in range(HT):
                    done = nc.tensor.matmul(wide[CT][:], ba_col[:, h:h + 1].broadcast_to([P, P]), wo_stage[:, h, :],
                                            start=(h == 0), stop=(h == HT - 1))
                done.then_inc(bao_done, 1)

            pe.wait_ge(ident_made, 2)
            pe.wait_ge(wa_loaded, 16)
            for h in range(HT):
                transposes(wide[h], [wa_stage[:, d, h * P:(h + 1) * P] for d in range(CT)]).then_inc(waT_done, 1)
            for d in range(CT):
                turn_c(0, d)
            pe.wait_ge(columns_loaded, 16 * 6)
            nc.tensor.matmul(score[0][:, 0:HT], ones[:], ba_col[:], start=True, stop=True)
            nc.tensor.matmul(score[0][:, HT:2 * HT], ones[:], bt_col[:], start=True, stop=True).then_inc(b_spread, 1)
            pe.wait_ge(wa_split, CT)

            def step(i, odd, first=False, last=False):
                j = i - 1
                project_k(i, 0)
                if not first:
                    turn_p(j, 0)
                project_k(i, 1)
                if not first:
                    turn_p(j, 1)
                    pe.wait_ge(pT_split, NB * j + 1)
                turn_x(i, 0)
                project_k(i, 2)
                if not first:
                    pe.wait_ge(pT_split, NB * j + 2)
                turn_x(i, 1)
                pe.wait_ge(xT_split, DT * i + 1)
                turn_x(i, 2)
                project_k(i, 3)
                pe.wait_ge(xT_split, DT * i + 2)
                turn_x(i, 3)
                if first:
                    pe.wait_ge(wt_split, DT)
                project_q(i, 0)
                turn_sum(i, turn[0], k_summed, k_sum_turned)
                project_q(i, 1)
                spread_rs(i, turn[0], k_rs, k_rstd, k_rs_spread)
                project_q(i, 2)
                project_q(i, 3)
                if first:
                    fold_weights(0)
                else:
                    probs_context(j, 0)
                    probs_context(j, 1)
                turn_sum(i, turn[1], q_summed, q_sum_turned)
                if first:
                    fold_weights(1)
                else:
                    pe.wait_ge(k_normed, HT * (i + 1))
                    probs_context(j, 2)
                    pe.wait_ge(q_centred, HT * i + 2)
                    output_part(j, 0, 0)
                    output_part(j, 0, 1)
                    output_part(j, 1, 0)
                spread_rs(i, turn[1], q_rs, q_rstd, q_rs_spread)
                if not first:
                    output_part(j, 0, 2)
                    output_part(j, 1, 1)
                    output_part(j, 1, 2)
                    for t in range(2, T - 1 if last else T):
                        pe.wait_ge(q_centred, HT * i + t + 1)
                        output(j, t)
                if first:
                    fold_weights(2)
                    fold_bias()
                if not last:
                    pe.wait_ge(k_normed, HT * (i + 1))
                    turn_c(i + 1, 0)
                    pe.wait_ge(q_normed, HT * (i + 1))
                    turn_c(i + 1, 1)
                pe.wait_ge(kT_split, HT * (i + 1))
                scores(i, 0, 0)
                if not last:
                    pe.wait_ge(cT_split, CT * (i + 1) + 1)
                    turn_c(i + 1, 2)
                scores(i, 0, 1)
                scores(i, 1, 0)
                scores(i, 1, 1)
                if first:
                    pe.wait_ge(wao_split, CT)
                    pe.wait_ge(bao_made, 1)

            run_steps(pe, step)
            turn_p(N - 1, 0)
            pe.wait_ge(q_centred, HT * N)
            output(N - 2, T - 1)
            turn_p(N - 1, 1)
            for b in range(NB):
                for d in range(CT):
                    if b == 0 and d == 2:
                        pe.wait_ge(pT_split, NB * (N - 1) + 1)
                    probs_context(N - 1, d, range(b, b + 1))
            for t in range(T):
                output(N - 1, t)

        @block.scalar
        def _(act):
            def xT_high(i, d):
                act.wait_ge(xT_done, DT * i + d + 1)
                wait(act, q_done, T * i)
                nc.scalar.copy(xT_hi[:, d, :], turn[d % 2][:]).then_inc(xT_hi_made, 1)

            def cT_high(i, d):
                act.wait_ge(cT_done, CT * i + d + 1)
                wait(act, k_done, T * i)
                of = score[1] if d == 2 and isinstance(i, int) and i == 0 else turn[d % 2]
                nc.scalar.copy(cT_hi[:, d, :], of[:]).then_inc(cT_hi_made, 1)

            def pT_high(j, b):
                act.wait_ge(pT_done, NB * j + b + 1)
                wait(act, pc_done, CT * j)
                nc.scalar.copy(pT_hi[:, b, :], turn[b][:]).then_inc(pT_hi_made, 1)

            def pc_high(j, d):
                act.wait_ge(pc_done, CT * j + d + 1)
                wait(act, out_done, T * j)
                of = (score[0], score[1], turn[0])[d]
                nc.scalar.copy(pcT_hi[:, d, :], of[:]).then_inc(pc_hi_made, 1)

            def centre(to, h, bias, done, i, centred, squared):
                act.wait_ge(done, HT * i + h + 1)
                nc.scalar.activation(squares[:, h, :], wide[h][:], ACT.Square, bias=bias[:, h:h + 1]).then_inc(squared, 1)
                nc.scalar.activation(to[:, h, :], wide[h][:], ACT.Identity, bias=bias[:, h:h + 1]).then_inc(centred, 1)

            def k_centre(i, h):
                wait(act, kT_split, HT * (i - 1) + h + 1)
                wait(act, q_summed, i)
                centre(k_cols, h, bac_col, k_done, i, k_centred, k_squared)

            def q_centre(i, h):
                wait(act, qT_split, HT * (i - 1) + h + 1)
                act.wait_ge(k_summed, i + 1)
                centre(q_cols, h, btc_col, q_done, i, q_centred, q_squared)

            def k_high(i, h):
                act.wait_ge(k_normed, HT * i + h + 1)
                nc.scalar.activation(kT_hi[:, h, :], k_cols[:, h, :], ACT.Identity,
                                     bias=beta2_col[:, h:h + 1]).then_inc(kT_hi_made, 1)

            def q_high(i, h):
                act.wait_ge(q_normed, HT * i + h + 1)
                nc.scalar.activation(qT_hi[:, h, :], q_cols[:, h, :], ACT.Identity,
                                     bias=beta1_col[:, h:h + 1]).then_inc(qT_hi_made, 1)

            def y_norm(j, odd, t):
                act.wait_ge(y_scales, T * j + t + 1)
                nc.scalar.activation(y_rows[odd][:, t, :], y_rows[odd][:, t, :], ACT.Identity,
                                     scale=y_sc[:, t, 0:1], bias=y_sc[:, t, 1:2]).then_inc(y_normed, 1)

            def exponentials(i, b):
                act.wait_ge(neg_max_made, NB * i + b + 1)
                wait(act, pT_done, NB * (i - 1) + b + 1)
                wait(act, sums_inverted, i)
                for l in range(LT):
                    at = LT * b + l
                    nc.scalar.activation(probs[:, at, :], score[b][:, l * S:(l + 1) * S], ACT.Exp,
                                         scale=SCALE, bias=neg_max[:, at:at + 1],
                                         accum_out=row_sum[:, at:at + 1]).then_inc(probs_made, 1)

            def wao_high(d):
                act.wait_ge(wao_done, d + 1)
                nc.scalar.copy(wao_hi[:, d, :], wide[d][:]).then_inc(wao_hi_made, 1)

            def wa_high():
                act.wait_ge(wa_mean_made, 1)
                for d in range(CT):
                    nc.scalar.activation(wa_hi[:, d, :], wa_stage[:, d, :], ACT.Identity,
                                         bias=wa_mean[:, d:d + 1]).then_inc(wa_hi_made, 1)

            def waT_copy(h):
                act.wait_ge(waT_done, h + 1)
                nc.scalar.copy(waT_stage[:, h, 0:DC], wide[h][:, 0:DC]).then_inc(waT_copied, 1)

            waT_copy(0)
            waT_copy(1)
            wa_high()
            for d in range(CT):
                cT_high(0, d)
            waT_copy(2)
            waT_copy(3)
            act.wait_ge(wa_split, CT)
            act.wait_ge(b_centred, 2)

            def step(i, odd, first=False, last=False):
                j = i - 1
                if not first:
                    pT_high(j, 0)
                k_centre(i, 0)
                if not isinstance(i, int) or i >= 2:
                    y_norm(i - 2, odd, 2)
                if not first:
                    pT_high(j, 1)
                xT_high(i, 0)
                k_centre(i, 1)
                k_centre(i, 2)
                xT_high(i, 1)
                xT_high(i, 2)
                if not isinstance(i, int) or i >= 2:
                    y_norm(i - 2, odd, 3)
                xT_high(i, 3)
                k_centre(i, 3)
                if first:
                    act.wait_ge(wt_split, DT)
                q_centre(i, 0)
                q_centre(i, 1)
                k_high(i, 0)
                k_high(i, 1)
                q_centre(i, 2)
                k_high(i, 2)
                k_high(i, 3)
                q_centre(i, 3)
                if first:
                    wao_high(0)
                    wao_high(1)
                else:
                    for d in range(CT):
                        pc_high(j, d)
                for h in range(HT):
                    q_high(i, h)
                if first:
                    wao_high(2)
                if not last:
                    cT_high(i + 1, 0)
                    cT_high(i + 1, 1)
                    cT_high(i + 1, 2)
                if not first:
                    y_norm(j, 1 - odd, 0)
                exponentials(i, 0)
                if not first:
                    y_norm(j, 1 - odd, 1)
                exponentials(i, 1)

            run_steps(act, step)
            for b in range(NB):
                pT_high(N - 1, b)
            y_norm(N - 2, 0, 2)
            for d in range(CT):
                pc_high(N - 1, d)
            y_norm(N - 2, 0, 3)
            for t in range(T):
                y_norm(N - 1, 1, t)

        @block.vector
        def _(dve):
            def low(to, whole, hi):
                return nc.vector.tensor_tensor(to, whole, hi.bitcast(F32), ALU.subtract)

            def xT_low(i, d):
                dve.wait_ge(xT_hi_made, DT * i + d + 1)
                low(xT_lo[:, d, :], turn[d % 2][:], xT_hi[:, d, :]).then_inc(xT_split, 1)

            def cT_low(i, d):
                dve.wait_ge(cT_hi_made, CT * i + d + 1)
                of = score[1] if d == 2 and isinstance(i, int) and i == 0 else turn[d % 2]
                low(cT_lo[:, d, :], of[:], cT_hi[:, d, :]).then_inc(cT_split, 1)

            def pT_low(j, b):
                dve.wait_ge(pT_hi_made, NB * j + b + 1)
                low(pT_lo[:, b, :], turn[b][:], pT_hi[:, b, :]).then_inc(pT_split, 1)

            def pc_low(j, d):
                dve.wait_ge(pc_hi_made, CT * j + d + 1)
                of = (score[0], score[1], turn[0])[d]
                low(pcT_lo[:, d, :], of[:], pcT_hi[:, d, :]).then_inc(pc_split, 1)

            def add_square(i, paired, squared, added):
                dve.wait_ge(paired, i + 1)
                dve.wait_ge(squared, HT * i + 3)
                nc.vector.tensor_tensor(squares[:, 2, :], squares[:, 0, :], squares[:, 2, :],
                                        ALU.add).then_inc(added, 1)

            def sum_squares(i, squared, added, summed, sum_turned, before):
                wait(dve, sum_turned, before)
                dve.wait_ge(added, i + 1)
                dve.wait_ge(squared, HT * (i + 1))
                nc.vector.tensor_tensor(square_sum[:], squares[:, 2, :], squares[:, 3, :],
                                        ALU.add).then_inc(summed, 1)

            def sum_rows(i, of, turned, ssq, made):
                dve.wait_ge(turned, i + 1)
                nc.vector.reduce_sum(ssq[:], of[:].rearrange("p (t f) -> p t f", t=T), AX_X).then_inc(made, 1)

            def norm(i, h, rs, cols, gain, centred, spread, normed):
                if h == 0:
                    dve.wait_ge(spread, i + 1)
                dve.wait_ge(centred, HT * i + h + 1)
                nc.vector.scalar_tensor_tensor(out=cols[:, h, :], in0=cols[:, h, :], scalar=gain[:, h:h + 1],
                                               in1=rs[:], op0=ALU.mult, op1=ALU.mult).then_inc(normed, 1)

            def shifted_low(i, h, lo, hi, cols, shift, hi_made, split):
                dve.wait_ge(hi_made, HT * i + h + 1)
                nc.vector.scalar_tensor_tensor(out=lo[:, h, :], in0=cols[:, h, :], scalar=shift[:, h:h + 1],
                                               in1=hi[:, h, :].bitcast(F32), op0=ALU.add,
                                               op1=ALU.subtract).then_inc(split, 1)

            def k_norm(i, h):
                norm(i, h, turn[0], k_cols, g2_col, k_centred, k_rs_spread, k_normed)

            def q_norm(i, h):
                norm(i, h, turn[1], q_cols, g1_col, q_centred, q_rs_spread, q_normed)

            def k_low(i, h):
                shifted_low(i, h, kT_lo, kT_hi, k_cols, beta2_col, kT_hi_made, kT_split)

            def q_low(i, h):
                shifted_low(i, h, qT_lo, qT_hi, q_cols, beta1_col, qT_hi_made, qT_split)

            def y_sum(j, odd, t):
                dve.wait_ge(out_done, T * j + t + 1)
                dve.wait_ge(x_biased, T * j + t + 1)
                dve.wait_ge(sums_inverted, j + 1)
                rows = y_rows[odd][:, t, :]
                nc.vector.scalar_tensor_tensor(out=rows, in0=wide[t][:], scalar=row_inv[:, t:t + 1],
                                               in1=rows, op0=ALU.mult, op1=ALU.add).then_inc(y_summed, 1)

            def y_stat(j, odd, t):
                dve.wait_ge(y_summed, T * j + t + 1)
                nc.vector.bn_stats(y_bn[:, t, :], y_rows[odd][:, t, :]).then_inc(y_stats, 1)

            def y_moment(j, t):
                wait_apart(dve, y_stats, T * j + t + 1)
                nc.vector.bn_aggr(y_mv[:, t, :], y_bn[:, t, :]).then_inc(y_moments, 1)

            def maxima(i, b):
                tiles = slice(LT * b, LT * (b + 1))
                dve.wait_ge(score_done, NB * i + b + 1)
                nc.vector.reduce_max(row_max[:, tiles], score[b][:].rearrange("p (l s) -> p l s", l=LT),
                                     AX_X).then_inc(max_made, 1)
                dve.wait_ge(max_made, NB * i + b + 1)
                nc.vector.tensor_scalar(neg_max[:, tiles], row_max[:, tiles], -SCALE, None,
                                        ALU.mult).then_inc(neg_max_made, 1)

            def invert_sums(j):
                dve.wait_ge(probs_made, T * (j + 1))
                nc.vector.reciprocal(row_inv[:], row_sum[:]).then_inc(sums_inverted, 1)

            def finish_last(t):
                rows = y_rows[1][:, t, :]
                dve.wait_ge(y_normed, T * (N - 1) + t + 1)
                nc.vector.tensor_tensor(rows, rows, go_row[:], ALU.mult).then_inc(last_scaled[1], 1)
                dve.wait_ge(last_scaled[1], max(t, 1))
                nc.vector.tensor_tensor(rows, rows, betao_row[:], ALU.add).then_inc(last_ready[1], 1)

            def weights_means(of, n, mean, summed, mean_made):
                nc.vector.reduce_sum(mean[:], of[:, 0:n, :], AX_X).then_inc(summed, 1)
                dve.wait_ge(summed, 1)
                nc.vector.tensor_scalar(mean[:], mean[:], -1.0 / H, None, ALU.mult).then_inc(mean_made, 1)

            def weights_low(to_lo, to_hi, of, d, mean, hi_made, split):
                dve.wait_ge(hi_made, d + 1)
                nc.vector.scalar_tensor_tensor(out=to_lo[:, d, :], in0=of[:, d, :], scalar=mean[:, d:d + 1],
                                               in1=to_hi[:, d, :].bitcast(F32), op0=ALU.add,
                                               op1=ALU.subtract).then_inc(split, 1)

            def wao_low(d):
                dve.wait_ge(wao_hi_made, d + 1)
                low(wao_lo[:, d, :], wide[d][:], wao_hi[:, d, :]).then_inc(wao_split, 1)

            def make_bao():
                dve.wait_ge(bao_done, 1)
                dve.wait_ge(rows_loaded, 16 * 3)
                nc.vector.tensor_tensor(bao_row[:], wide[CT][:], bao_row[:], ALU.add).then_inc(bao_made, 1)

            dve.wait_ge(wa_loaded, 16)
            weights_means(wa_stage, CT, wa_mean, wa_summed, wa_mean_made)
            for d in range(CT):
                weights_low(wa_lo, wa_hi, wa_stage, d, wa_mean, wa_hi_made, wa_split)
            for d in range(CT):
                cT_low(0, d)
            dve.wait_ge(b_spread, 1)
            nc.vector.reduce_sum(b_sum[:], score[0][:, 0:2 * HT].rearrange("p (n h) -> p n h", n=2),
                                 AX_X).then_inc(b_summed, 1)
            dve.wait_ge(b_summed, 1)
            nc.vector.tensor_scalar(b_mean[:], b_sum[:], -1.0 / H, None, ALU.mult).then_inc(b_mean_made, 1)
            dve.wait_ge(b_mean_made, 1)
            for n, (to, of) in enumerate(((bac_col, ba_col), (btc_col, bt_col))):
                nc.vector.tensor_scalar(to[:], of[:], b_mean[:, n:n + 1], None, ALU.add).then_inc(b_centred, 1)
            dve.wait_ge(wt_loaded, 16)
            weights_means(wt_stage, DT, wt_mean, wt_summed, wt_mean_made)

            def step(i, odd, first=False, last=False):
                j = i - 1
                if not first:
                    invert_sums(j)
                    pT_low(j, 0)
                    pT_low(j, 1)
                xT_low(i, 0)
                if first:
                    for d in range(DT):
                        weights_low(wt_lo, wt_hi, wt_stage, d, wt_mean, wt_hi_made, wt_split)
                xT_low(i, 1)
                xT_low(i, 2)
                add_square(i, k_paired, k_squared, k_added)
                xT_low(i, 3)
                sum_squares(i, k_squared, k_added, k_summed, q_sum_turned, i)
                sum_rows(i, turn[0], k_sum_turned, k_ssq, k_ssq_made)
                k_norm(i, 0)
                k_norm(i, 1)
                k_low(i, 0)
                k_norm(i, 2)
                k_norm(i, 3)
                k_low(i, 1)
                add_square(i, q_paired, q_squared, q_added)
                k_low(i, 2)
                sum_squares(i, q_squared, q_added, q_summed, k_sum_turned, i + 1)
                k_low(i, 3)
                if not first:
                    pc_low(j, 0)
                sum_rows(i, turn[1], q_sum_turned, q_ssq, q_ssq_made)
                if not first:
                    pc_low(j, 1)
                    pc_low(j, 2)
                if first:
                    wao_low(0)
                    wao_low(1)
                q_norm(i, 0)
                q_norm(i, 1)
                q_low(i, 0)
                q_norm(i, 2)
                q_low(i, 1)
                q_norm(i, 3)
                q_low(i, 2)
                q_low(i, 3)
                if first:
                    wao_low(2)
                    make_bao()
                if not first:
                    y_sum(j, 1 - odd, 0)
                    y_sum(j, 1 - odd, 1)
                if not last:
                    cT_low(i + 1, 0)
                if not first:
                    y_stat(j, 1 - odd, 0)
                    y_stat(j, 1 - odd, 1)
                    y_moment(j, 0)
                if not last:
                    cT_low(i + 1, 1)
                if not first:
                    y_moment(j, 1)
                    y_sum(j, 1 - odd, 2)
                    if not last:
                        y_sum(j, 1 - odd, 3)
                if not last:
                    cT_low(i + 1, 2)
                maxima(i, 0)
                maxima(i, 1)
                if not first:
                    y_stat(j, 1 - odd, 2)
                    if not last:
                        y_stat(j, 1 - odd, 3)
                    y_moment(j, 2)
                    if not last:
                        y_moment(j, 3)

            run_steps(dve, step)
            pT_low(N - 1, 0)
            y_sum(N - 2, 0, 3)
            pT_low(N - 1, 1)
            dve.wait_ge(y_summed, T * (N - 1))
            invert_sums(N - 1)
            y_stat(N - 2, 0, 3)
            y_moment(N - 2, 3)
            for d in range(CT):
                pc_low(N - 1, d)
            for t in range(T):
                y_sum(N - 1, 1, t)
                y_stat(N - 1, 1, t)
                if t == 3:
                    dve.wait_ge(y_scales, T * (N - 1))
                y_moment(N - 1, t)
            for t in (0, 2, 3):
                finish_last(t)

        @block.gpsimd
        def _(pool):
            def scales(i, t, moments, mv, sc, var, rstd, made):
                at = T * i + t + 1
                wait_apart(pool, moments, at)
                nc.gpsimd.tensor_scalar(sc[:, t, 2:3], mv[:, t, 1:2], EPS, 1.0, ALU.add, ALU.mult).then_inc(var, 1)
                pool.wait_ge(var, at)
                nc.gpsimd.tensor_tensor(sc[:, t, 0:1], sc[:, t, 2:3], neg_half[:, 0:1], ALU.pow).then_inc(rstd, 1)
                wait_apart(pool, rstd, at)
                nc.gpsimd.tensor_scalar(sc[:, t, 1:2], mv[:, t, 0:1], sc[:, t, 0:1], neg_one[:, 0:1],
                                        ALU.mult, ALU.mult).then_inc(made, 1)

            def pair_squares(i, squared, paired):
                pool.wait_ge(squared, HT * i + 2)
                nc.gpsimd.tensor_tensor(squares[:, 0, :], squares[:, 0, :], squares[:, 1, :],
                                        ALU.add).then_inc(paired, 1)

            def row_rstd(i, ssq_made, ssq, ve, rs, var, rstd):
                wait_apart(pool, ssq_made, i + 1)
                nc.gpsimd.tensor_scalar(ve[:], ssq[:], 1.0 / H, EPS, ALU.mult, ALU.add).then_inc(var, 1)
                pool.wait_ge(var, i + 1)
                nc.gpsimd.tensor_tensor(rs[:], ve[:], neg_half[:], ALU.pow).then_inc(rstd, 1)

            def y_scale(j, t):
                scales(j, t, y_moments, y_mv, y_sc, y_var, y_rstd, y_scales)

            def split_c(i, t):
                if t == 0:
                    wait_apart(pool, c_copied, 16 * (i + 1))
                    wait_apart(pool, pc_done, CT * i)
                nc.gpsimd.tensor_scalar(c_hi[:, t, :], c_kept[:, t, :], 1.0, 1.0, ALU.mult,
                                        ALU.mult).then_inc(c_hi_made, 1)
                pool.wait_ge(c_hi_made, T * i + t + 1)
                nc.gpsimd.tensor_tensor(c_lo[:, t, :], c_kept[:, t, :], c_hi[:, t, :].bitcast(F32),
                                        ALU.subtract).then_inc(c_split, 1)

            def bias_x(i, odd, t):
                if t == 0:
                    pool.wait_ge(x_loaded, 16 * T * (i + 1))
                wait(pool, stored[t], 16 * (i - 1))
                nc.gpsimd.tensor_tensor(y_rows[odd][:, t, :], x_in[:, t, :], bao_row[:], ALU.add).then_inc(x_biased, 1)

            def finish_y(j, odd, t):
                rows = y_rows[odd][:, t, :]
                pool.wait_ge(y_normed, T * j + t + 1)
                nc.gpsimd.tensor_tensor(rows, rows, go_row[:], ALU.mult).then_inc(y_scaled, 1)
                pool.wait_ge(y_scaled, T * j + t + 1)
                nc.gpsimd.tensor_tensor(rows, rows, betao_row[:], ALU.add).then_inc(y_ready, 1)

            def finish_last(t):
                rows = y_rows[1][:, t, :]
                pool.wait_ge(y_normed, T * (N - 1) + t + 1)
                nc.gpsimd.tensor_tensor(rows, rows, go_row[:], ALU.mult).then_inc(last_scaled[0], 1)
                pool.wait_ge(last_scaled[0], 1)
                nc.gpsimd.tensor_tensor(rows, rows, betao_row[:], ALU.add).then_inc(last_ready[0], 1)

            nc.gpsimd.memset(ident[:], 0.0).then_inc(ident_zeroed, 1)
            nc.gpsimd.memset(neg_half[:], -0.5).then_inc(ident_zeroed, 1)
            nc.gpsimd.memset(neg_one[:], -1.0).then_inc(ident_zeroed, 1)
            pool.wait_ge(ident_zeroed, 3)
            nc.gpsimd.affine_select(out=ident[:], in_=ident[:], compare_op=ALU.not_equal, fill=1.0, base=0,
                                    pattern=[[-1, P]], channel_multiplier=1).then_inc(ident_made, 1)
            nc.gpsimd.memset(ones[:], 1.0).then_inc(ident_made, 1)
            pool.wait_ge(wt_mean_made, 1)
            for d in range(DT):
                nc.gpsimd.tensor_scalar(wt_hi[:, d, :], wt_stage[:, d, :], wt_mean[:, d:d + 1], 1.0, ALU.add,
                                        ALU.mult).then_inc(wt_hi_made, 1)

            def step(i, odd, first=False, last=False):
                j = i - 1
                pair_squares(i, k_squared, k_paired)
                if not isinstance(i, int) or i >= 2:
                    finish_y(i - 2, odd, 2)
                    finish_y(i - 2, odd, 3)
                row_rstd(i, k_ssq_made, k_ssq, k_ve, k_rs, k_var, k_rstd)
                if not first:
                    bias_x(i, odd, 0)
                    bias_x(i, odd, 1)
                pair_squares(i, q_squared, q_paired)
                if not first:
                    bias_x(i, odd, 2)
                    bias_x(i, odd, 3)
                row_rstd(i, q_ssq_made, q_ssq, q_ve, q_rs, q_var, q_rstd)
                if first:
                    pool.wait_ge(bao_made, 1)
                    pool.wait_ge(wao_done, CT)
                    for t in range(T):
                        bias_x(i, odd, t)
                for t in range(T):
                    split_c(i, t)
                if not first:
                    y_scale(j, 0)
                    y_scale(j, 1)
                    finish_y(j, 1 - odd, 0)
                    y_scale(j, 2)
                    y_scale(j, 3)
                    finish_y(j, 1 - odd, 1)

            run_steps(pool, step)
            for t in (2, 3):
                finish_y(N - 2, 0, t)
            for t in range(T):
                y_scale(N - 1, t)
            finish_last(1)


_INS = ["x", "ctx_768", "L0_xattn_W_text", "L0_xattn_b_text", "L0_xattn_W_audio", "L0_xattn_b_audio",
        "L0_xattn_W_out", "L0_xattn_b_out", "L0_xattn_g1", "L0_xattn_beta1", "L0_xattn_g2", "L0_xattn_beta2",
        "L0_xattn_g_out", "L0_xattn_beta_out"]


def kernel(**inputs):
    import numpy as _np
    import concourse.bacc as _bacc
    from concourse import mybir as _mybir
    from concourse.bass_utils import run_bass_kernel_spmd as _run

    nc = _bacc.Bacc("TRN2", target_bir_lowering=False, num_devices=1)
    arrays, args = {}, []
    for name in _INS:
        a = _np.ascontiguousarray(inputs[name])
        arrays[f"in_{name}"] = a
        args.append(nc.dram_tensor(f"in_{name}", a.shape, _mybir.dt.from_np(a.dtype), kind="ExternalInput").ap())
    out = nc.dram_tensor("out", arrays["in_x"].shape, _mybir.dt.float32, kind="ExternalOutput").ap()
    cross_attention_kernel(nc, *args, out)
    r = _run(nc, [arrays], core_ids=[0])
    return r.results[0]["out"]
```
